# Optimizing a Trainium2 kernel written in Bass

```python
import numpy as np
import jax
import jax.numpy as jnp

def _softmax(x, axis=-1):
    return jax.nn.softmax(x, axis=axis)

def _gelu(x):
    return jax.nn.gelu(x, approximate=True)

def _silu(x):
    return jax.nn.silu(x)

def _sigmoid(x):
    return jax.nn.sigmoid(x)

def _layernorm(x, axis=-1, eps=1e-05):
    m = jnp.mean(x, axis=axis, keepdims=True)
    v = jnp.var(x, axis=axis, keepdims=True)
    return (x - m) / jnp.sqrt(v + eps)

def _scatter_add(tgt, idx, src, axis=0):
    return tgt.at[idx].add(src)

def _segment_sum(src, seg, n):
    return jax.ops.segment_sum(src, seg, n)
kernel_name = 'mk_cond_seq_d2_seqx_r4_c5be8f'

def setup_inputs(seed: int=0):
    np.random.seed(seed)
    _w = jnp.asarray

    def _rec_inputs():
        import jax
        import jax.numpy as jnp
        _rk = jax.random.key(seed)
        x = -0.0003929 + 0.9999 * jax.random.normal(jax.random.fold_in(_rk, 1), (64, 64, 256), jnp.float32)
        _lenS = 64 - jax.random.randint(jax.random.fold_in(_rk, 7), (64,), 0, max(1, 64 // 4) + 1, jnp.int32)
        _lenS2 = 64 - jax.random.randint(jax.random.fold_in(_rk, 8), (64,), 0, max(1, 64 // 4) + 1, jnp.int32)
        cond_256 = -0.0209273 + 1.04763 * jax.random.normal(jax.random.fold_in(_rk, 11), (64, 64), jnp.float32)
        return (x, cond_256)
    x, cond_256 = _rec_inputs()

    def _L0_cond_setup():
        import jax, jax.numpy as jnp
        import numpy as np
        EPS = 1e-06

        def act_quant(x):
            scale = 127.0 / jnp.clip(jnp.max(jnp.abs(x), axis=-1, keepdims=True), 1e-05, None)
            return jnp.clip(jnp.round(x * scale), -128.0, 127.0) / scale

        def weight_quant(w):
            scale = 1.0 / jnp.clip(jnp.mean(jnp.abs(w)), 1e-05, None)
            return jnp.clip(jnp.round(w * scale), -1.0, 1.0) / scale
        key = jax.random.key(seed)
        k0, k1, k2, k3, k4 = jax.random.split(key, 5)
        B, S, D, FF, C = (4, 1024, 256, 1024, 64)
        return {'x': jax.random.normal(k0, (B, S, D), jnp.float32), 'cond': jax.random.normal(k1, (B, C), jnp.float32), 'norm_w': jax.random.normal(k2, (D, C), jnp.float32) * 0.02, 'up_w': jax.random.normal(k3, (2 * FF, D), jnp.float32) * 0.02, 'down_w': jax.random.normal(k4, (D, FF), jnp.float32) * 0.02}
    _L0_cond_all = _L0_cond_setup()
    _L0_cond_in = {k: v for k, v in _L0_cond_all.items() if k in ('norm_w', 'up_w', 'down_w')}
    del _L0_cond_all

    def _L1_cond_setup():
        import jax, jax.numpy as jnp
        import numpy as np
        DIM = 256
        BN = 128
        H = 64
        DELTA_SCALE = 0.1
        key = jax.random.key(seed)
        ks = jax.random.split(key, 10)
        B, L = (16, 512)

        def init(k, shape, fan_in):
            bound = 1.0 / np.sqrt(fan_in)
            return jax.random.uniform(k, shape, jnp.float32, -bound, bound)
        return {'x': jax.random.normal(ks[0], (B, L, DIM), jnp.float32), 'h_lang': jax.random.normal(ks[1], (B, H), jnp.float32), 'Wd': init(ks[2], (BN, DIM), DIM), 'bd': init(ks[3], (BN,), DIM), 'Wu': init(ks[4], (DIM, BN), BN), 'bu': init(ks[5], (DIM,), BN), 'Wdd': init(ks[6], (BN * DIM, H), H), 'bdd': init(ks[7], (BN * DIM,), H), 'Wdu': init(ks[8], (DIM * BN, H), H), 'bdu': init(ks[9], (DIM * BN,), H)}
    _L1_cond_all = _L1_cond_setup()
    _L1_cond_in = {k: v for k, v in _L1_cond_all.items() if k in ('Wd', 'bd', 'Wu', 'bu', 'Wdd', 'bdd', 'Wdu', 'bdu')}
    del _L1_cond_all
    return {'x': x, 'cond_256': cond_256, 'L0_cond_norm_w': _L0_cond_in['norm_w'], 'L0_cond_up_w': _L0_cond_in['up_w'], 'L0_cond_down_w': _L0_cond_in['down_w'], 'L1_cond_Wd': _L1_cond_in['Wd'], 'L1_cond_bd': _L1_cond_in['bd'], 'L1_cond_Wu': _L1_cond_in['Wu'], 'L1_cond_bu': _L1_cond_in['bu'], 'L1_cond_Wdd': _L1_cond_in['Wdd'], 'L1_cond_bdd': _L1_cond_in['bdd'], 'L1_cond_Wdu': _L1_cond_in['Wdu'], 'L1_cond_bdu': _L1_cond_in['bdu']}

def reference(x, cond_256, L0_cond_norm_w, L0_cond_up_w, L0_cond_down_w, L1_cond_Wd, L1_cond_bd, L1_cond_Wu, L1_cond_bu, L1_cond_Wdd, L1_cond_bdd, L1_cond_Wdu, L1_cond_bdu):
    import jax
    import jax.numpy as jnp

    def _L0_cond_ref(x, cond, norm_w, up_w, down_w):
        import jax, jax.numpy as jnp
        import numpy as np
        EPS = 1e-06

        def act_quant(x):
            scale = 127.0 / jnp.clip(jnp.max(jnp.abs(x), axis=-1, keepdims=True), 1e-05, None)
            return jnp.clip(jnp.round(x * scale), -128.0, 127.0) / scale

        def weight_quant(w):
            scale = 1.0 / jnp.clip(jnp.mean(jnp.abs(w)), 1e-05, None)
            return jnp.clip(jnp.round(w * scale), -1.0, 1.0) / scale
        scale = cond @ norm_w.T + 1.0
        ms = jnp.mean(x * x, axis=-1, keepdims=True)
        h = x * (scale[:, None, :] * jax.lax.rsqrt(ms + EPS))
        u = h @ up_w.T
        val, gate = jnp.split(u, 2, axis=-1)
        h = val * jax.nn.gelu(gate, approximate=False)
        hq = h + jax.lax.stop_gradient(act_quant(h) - h)
        wq = down_w + jax.lax.stop_gradient(weight_quant(down_w) - down_w)
        y = hq @ wq.T
        return y + x

    def _L1_cond_ref(x, h_lang, Wd, bd, Wu, bu, Wdd, bdd, Wdu, bdu):
        import jax, jax.numpy as jnp
        import numpy as np
        DIM = 256
        BN = 128
        H = 64
        DELTA_SCALE = 0.1
        B, L, D = x.shape
        dWd = ((h_lang @ Wdd.T + bdd) * DELTA_SCALE).reshape(B, BN, D)
        dWu = ((h_lang @ Wdu.T + bdu) * DELTA_SCALE).reshape(B, D, BN)
        Wd_b = Wd + dWd
        Wu_b = Wu + dWu
        down = jax.nn.relu(jnp.einsum('bld,bnd->bln', x, Wd_b) + bd)
        up = jnp.einsum('bln,bdn->bld', down, Wu_b) + bu
        return x + up
    x = _L0_cond_ref(x, cond_256, L0_cond_norm_w, L0_cond_up_w, L0_cond_down_w)
    x = _L1_cond_ref(x, cond_256, L1_cond_Wd, L1_cond_bd, L1_cond_Wu, L1_cond_bu, L1_cond_Wdd, L1_cond_bdd, L1_cond_Wdu, L1_cond_bdu)
    return x

_drawn_inputs = setup_inputs


def setup_inputs(seed=0):
    import zlib

    import numpy as np

    out = dict(_drawn_inputs(seed))
    spreads = {}
    factors = {'L0_cond_norm_w': 8.0, 'L1_cond_bd': 3.165}
    for name, (base, spread) in spreads.items():
        noise = np.random.default_rng([zlib.crc32(name.encode()), seed]).standard_normal(out[name].shape)
        drawn = base * np.exp(spread * noise) if base else spread * noise
        out[name] = jnp.asarray(drawn.astype(out[name].dtype))
    for name, factor in factors.items():
        out[name] = (out[name] * factor).astype(out[name].dtype)
    return out
```

```python
from contextlib import ExitStack

import concourse.bass as bass
from concourse import mybir
from concourse.alu_op_type import AluOpType as ALU

ACT = mybir.ActivationFunctionType
AX = mybir.AxisListType
F32 = mybir.dt.float32
F32R = mybir.dt.float32r
BF16 = mybir.dt.bfloat16

P = 128
BATCH, SEQ, D, C = 64, 64, 256, 64
FF, BN = 1024, 128
TILES = BATCH * SEQ // P
K = D // P
PER = P // SEQ
FC = FF // P
HALF = FF // 2
ROWS = 4
CHUNKS = 2 * BN // ROWS
EARLY = 16
SLOTS = 3
PAIRS = TILES // 2
RING = 4
ROUND = 12582912.0
QMAX = 127.0
DELTA = 0.1
EPS = 1e-6
TINY = 1e-5
assert EARLY + SLOTS * PAIRS == CHUNKS


def slot_of(q):
    return (q + SLOTS - EARLY % SLOTS) % SLOTS


def use_of(q):
    return sum(slot_of(x) == slot_of(q) for x in range(q))


def after(engine, semaphore, value):
    if not isinstance(value, int) or value > 0:
        engine.wait_ge(semaphore, value)


def build(nc, x, x_t, cond_t, norm_t, up_t, down_t, gen_w, base_w, base_b, down_bias, up_bias, out):
    scratch = nc.dram_tensor("layer1_weights", [BATCH, K, 2, P, P], F32, kind="Internal").ap()

    with ExitStack() as ctx:
        def sb(name, shape, dt=F32):
            return ctx.enter_context(nc.sbuf_tensor(name, shape, dt))

        def sem(name):
            return ctx.enter_context(nc.semaphore(name))

        x1 = sb("x1", [P, TILES, D])
        up_raw = sb("up_raw", [P, K, 2 * FF])
        up_hi = sb("up_hi", [P, K, 2 * FF], F32R)
        up_lo = sb("up_lo", [P, K, 2 * FF], F32R)
        down_raw = sb("down_raw", [P, FC, D])
        down_q = sb("down_q", [P, FC, D], BF16)
        norm_sb = sb("norm_sb", [C, D])
        scale_t = sb("scale_t", [P, K, BATCH])
        xt_in = sb("xt_in", [P, 2, K, P])
        h_all = sb("h_all", [P, K, P])
        h_hi = sb("h_hi", [P, 2, K, P], F32R)
        h_lo = sb("h_lo", [P, 2, K, P], F32R)
        gelu = sb("gelu", [P, 2, HALF])
        hid = sb("hid", [P, FF])
        quant = sb("quant", [P, FF], BF16)
        quant_t = sb("quant_t", [P, FC, P], BF16)
        square = sb("square", [P, D])
        sumsq = sb("sumsq", [P, 2])
        rms = sb("rms", [P, 2, 5])
        peak = sb("peak", [P, 2, 4])
        factor = sb("factor", [P, 2])
        numbers = sb("numbers", [P, 3])
        weight_sum = sb("weight_sum", [P, 4])
        ident_b = sb("ident_b", [P, P], BF16)
        ident = sb("ident", [P, P])
        ones = sb("ones", [P, P])
        cond2 = sb("cond2", [P, P])
        chunk_in = sb("chunk_in", [P, SLOTS, ROWS * P])
        chunk_out = sb("chunk_out", [P, SLOTS, ROWS * P])
        base = sb("base", [P, K, 2, P])
        base_raw = sb("base_raw", [P, 2, K, 2, P])
        delta_in = sb("delta_in", [P, RING, PER, K, 2, P])
        w1 = sb("w1", [P, RING, PER, K, 2, P])
        x1_tile = sb("x1_tile", [P, RING, D])
        x1_t = sb("x1_t", [P, 2, K, P])
        down_sb = sb("down_sb", [P, 2, P])
        down_relu = sb("down_relu", [P, 2, P])
        x1_bias = sb("x1_bias", [P, 2, D])
        out_sb = sb("out_sb", [P, 2, D])
        down_bias_sb = sb("down_bias_sb", [P, 1])
        up_bias_sb = sb("up_bias_sb", [P, D])

        banks = [ctx.enter_context(nc.psum_tensor(f"bank{i}", [P, HALF], F32)) for i in range(4)]
        bank_t = ctx.enter_context(nc.psum_tensor("bank_t", [P, FC, P], BF16))
        bank_y = ctx.enter_context(nc.psum_tensor("bank_y", [P, HALF], F32))
        bank_g = [ctx.enter_context(nc.psum_tensor(f"bank_g{i}", [P, HALF], F32)) for i in range(2)]
        gate_ps, val_ps = [banks[0], banks[2]], [banks[1], banks[3]]
        y_ps = bank_y[:, 0:D]
        chunk_ps = [bank_g[0], bank_g[1], bank_g[0]]
        x1_t_ps = [banks[0], banks[1]]
        down_ps = [banks[2], banks[3]]
        turned_ps = [bank_y, bank_y]
        up_ps = [bank_g[0], bank_g[1]]

        cond_in, norm_in, down_in = sem("cond_in"), sem("norm_in"), sem("down_in")
        up_in = [sem(f"up_in{n}") for n in range(4)]
        x_first, x_rest, small_in = sem("x_first"), sem("x_rest"), sem("small_in")
        xt_here = [sem(f"xt_here{p}") for p in range(2)]
        cleared, identity_made, ones_made = sem("cleared"), sem("identity_made"), sem("ones_made")
        identf_made, numbers_made = sem("identf_made"), sem("numbers_made")
        scale_ready, scale_made = sem("scale_ready"), sem("scale_made")
        up_hi_made, up_lo_made = sem("up_hi_made"), sem("up_lo_made")
        weights_summed, weights_total = sem("weights_summed"), sem("weights_total")
        weight_steps, down_q_made = sem("weight_steps"), sem("down_q_made")
        base_steps = sem("base_steps")
        chunk_here = [sem(f"chunk_here{s}") for s in range(SLOTS)]
        chunk_stored = [sem(f"chunk_stored{s}") for s in range(SLOTS)]
        chunk_made, chunk_copied = sem("chunk_made"), sem("chunk_copied")
        h_scaled, h_hi_made, h_split = sem("h_scaled"), sem("h_hi_made"), sem("h_split")
        gate_ready, val_ready = sem("gate_ready"), sem("val_ready")
        squared, rms_steps = sem("squared"), sem("rms_steps")
        gelu_done, hid_made, peak_steps = sem("gelu_done"), sem("hid_made"), sem("peak_steps")
        hid_rounded, quant_made = sem("hid_rounded"), sem("quant_made")
        quant_turned, quant_copied = sem("quant_turned"), sem("quant_copied")
        y_ready, factor_made, x1_made = sem("y_ready"), sem("factor_made"), sem("x1_made")
        delta_here = [sem(f"delta_here{s}") for s in range(RING)]
        x1_here = [sem(f"x1_here{s}") for s in range(RING)]
        w1_made, x1_turned, x1_copied = sem("w1_made"), sem("x1_turned"), sem("x1_copied")
        down_ready, down_copied = sem("down_ready"), sem("down_copied")
        down_turned, relu_done = sem("down_turned"), sem("relu_done")
        up_ready, bias_added, out_made = sem("up_ready"), sem("bias_added"), sem("out_made")
        out_stored = [sem(f"out_stored{p}") for p in range(2)]

        RMS_STEPS, PEAK_STEPS = 7, 4
        PIECES = [(FF + 0, FF + HALF), (0, HALF), (FF + HALF, 2 * FF), (HALF, FF)]
        block = ctx.enter_context(nc.Block())

        def walk0(engine, step):
            for p in range(2):
                step(p, 0, p, first=(p == 0), last=False)
            with engine.Fori(1, PAIRS - 1) as pair:
                for p in range(2):
                    step(pair * 2 + p, pair, p, first=False, last=False)
            for p in range(2):
                step(TILES - 2 + p, PAIRS - 1, p, first=False, last=(p == 1))

        def walk1(engine, step, lag):
            for t in range(RING):
                step(t, 0, t % RING)
            with engine.Fori(1, TILES // RING) as four:
                for s in range(RING):
                    step(four * RING + s, four, s)
            for t in range(TILES, TILES + lag):
                step(t, TILES // RING, t % RING)

        def live(t, back):
            return not isinstance(t, int) or 0 <= t - back < TILES

        def chunk(pair, c):
            return EARLY + pair * SLOTS + c

        def chunk_use(pair, c):
            return pair + use_of(EARLY + c)

        @block.sync
        def _(sp):
            def load_chunk(q, s):
                sp.dma_start(chunk_in[:, s, :], gen_w[q]).then_inc(chunk_here[s], 16)

            def store_chunk(q, s, m, i):
                sp.wait_ge(chunk_copied, q + 1)
                target = scratch[:, :, m, bass.ds(i * ROWS, ROWS), :].rearrange("b k r c -> k b (r c)")
                sp.dma_start(target, chunk_out[:, s, :]).then_inc(chunk_stored[s], 16)

            def load_xt(t, p):
                sp.dma_start(xt_in[:, p], x_t[t]).then_inc(xt_here[p], 16)

            sp.wait_ge(cleared, 1)
            sp.dma_start(cond2[0:C, 0:BATCH], cond_t).then_inc(cond_in, 16)
            sp.dma_start(cond2[C:P, BATCH:P], cond_t).then_inc(cond_in, 16)
            for q in range(SLOTS):
                load_chunk(q, slot_of(q))
            sp.dma_start(norm_sb[:], norm_t).then_inc(norm_in, 16)
            for p in range(2):
                load_xt(p, p)
            for n, (a, b) in enumerate(PIECES):
                sp.dma_start(up_raw[:, :, a:b], up_t[:, :, a:b]).then_inc(up_in[n], 16)
                if n == 1:
                    sp.dma_start(x1[:, 0:2, :], x[0:2].rearrange("t p d -> p t d")).then_inc(x_first, 16)
            for q in range(EARLY):
                store_chunk(q, slot_of(q), 0, q)
                sp.wait_ge(chunk_made, q + 1)
                load_chunk(q + SLOTS, slot_of(q))
            sp.dma_start(down_raw[:], down_t).then_inc(down_in, 16)
            sp.dma_start(x1[:, 2:TILES, :], x[2:TILES].rearrange("t p d -> p t d")).then_inc(x_rest, 16)
            for target, source in ((base_raw[:, 0], base_w), (base_raw[:, 1], base_b),
                                   (down_bias_sb[:], down_bias), (up_bias_sb[:], up_bias.to_broadcast([P, D]))):
                sp.dma_start(target, source).then_inc(small_in, 16)

            def chunks0(t, pair, c, m, i, more):
                q = chunk(pair, c)
                store_chunk(q, c, m, i)
                if more:
                    sp.wait_ge(chunk_made, q + 1)
                    load_chunk(q + SLOTS, c)

            def step0(t, pair, p, m, i, more):
                for c in ((0, 1) if p == 0 else (2,)):
                    chunks0(t, pair, c, m, i + c, more)
                if more:
                    sp.wait_ge(h_split, t + 1)
                    load_xt(t + 2, p)

            turn = (CHUNKS // 2 - EARLY) // SLOTS
            with sp.Fori(0, turn) as pair:
                for p in range(2):
                    step0(pair * 2 + p, pair, p, 0, pair * SLOTS + EARLY, True)
            for p in range(2):
                for c in ((0, 1) if p == 0 else (2,)):
                    q = chunk(turn, c)
                    chunks0(2 * turn + p, turn, c, q // (CHUNKS // 2), q % (CHUNKS // 2), True)
                sp.wait_ge(h_split, 2 * turn + p + 1)
                load_xt(2 * turn + p + 2, p)
            with sp.Fori(turn + 1, PAIRS - 1) as pair:
                for p in range(2):
                    step0(pair * 2 + p, pair, p, 1, pair * SLOTS + EARLY - CHUNKS // 2, True)
            for p in range(2):
                step0(TILES - 2 + p, PAIRS - 1, p, 1, chunk(PAIRS - 1, 0) - CHUNKS // 2, False)

            for s in range(SLOTS):
                sp.wait_ge(chunk_stored[s], 16 * (use_of(EARLY + s) + PAIRS))
            sp.wait_ge(x1_made, TILES)

            def load1(t, four, s):
                sp.dma_start(delta_in[:, s].rearrange("p b k m c -> p (b k m) c"),
                             scratch[bass.ds(t * PER, PER)].rearrange("b k m r c -> r (b k m) c")
                             ).then_inc(delta_here[s], 16)
                sp.dma_start(x1_tile[:, s, :], x1[:, bass.ds(t, 1), :].rearrange("p t d -> p (t d)")
                             ).then_inc(x1_here[s], 16)

            def store1(t, p, count):
                sp.wait_ge(out_made, t + 1)
                sp.dma_start(out[t], out_sb[:, p, :]).then_inc(out_stored[p], 16)

            for s in range(RING):
                load1(s, 0, s)
            with sp.Fori(0, TILES // RING - 1) as four:
                for s in range(RING):
                    t = four * RING + s
                    sp.wait_ge(w1_made, t + 1)
                    sp.wait_ge(x1_turned, t + 1)
                    load1(t + RING, four, s)
                    store1(t, s % 2, 0)
            for t in range(TILES - RING, TILES):
                store1(t, t % 2, 0)
            for p in range(2):
                sp.wait_ge(out_stored[p], 16 * TILES // 2)

        @block.gpsimd
        def _(pool):
            pool.memset(cond2[:], 0.0).then_inc(cleared, 1)
            pool.memset(ident[:], 0.0).then_inc(cleared, 1)
            pool.wait_ge(cleared, 2)
            pool.affine_select(out=ident[:], in_=ident[:], compare_op=ALU.not_equal, fill=1.0, base=0,
                               pattern=[[-1, P]], channel_multiplier=1).then_inc(identf_made, 1)
            pool.wait_ge(identf_made, 1)
            pool.tensor_copy(ident_b[:], ident[:]).then_inc(identity_made, 1)
            pool.memset(ones[:], 1.0).then_inc(ones_made, 1)
            minus_half, eps, one_half = (numbers[:, n:n + 1] for n in range(3))
            for place, value in ((minus_half, -0.5), (eps, EPS), (one_half, 1.5)):
                pool.memset(place, value).then_inc(numbers_made, 1)
            pool.wait_ge(numbers_made, 3)

            def root(t, pair, p, first, last):
                v, guess, sq, fix, r = (rms[:, p, n:n + 1] for n in range(5))
                done = t * RMS_STEPS
                pool.wait_ge(squared, t + 1)
                if not isinstance(t, int) or t >= 2:
                    pool.wait_ge(peak_steps, (t - 1) * PEAK_STEPS)
                for n, (result, one, other, op) in enumerate((
                        (v, sumsq[:, p:p + 1], eps, ALU.add), (guess, v, minus_half, ALU.pow),
                        (sq, guess, guess, ALU.mult), (sq, sq, v, ALU.mult), (fix, sq, minus_half, ALU.mult),
                        (fix, fix, one_half, ALU.add), (r, guess, fix, ALU.mult))):
                    if n:
                        pool.wait_ge(rms_steps, done + n)
                    pool.tensor_tensor(result, one, other, op).then_inc(rms_steps, 1)

            walk0(pool, root)

            pool.wait_ge(small_in, 64)
            pool.tensor_scalar(base[:], base_raw[:, 1], DELTA, None, ALU.mult).then_inc(base_steps, 1)
            pool.wait_ge(base_steps, 1)
            pool.tensor_tensor(base[:], base[:], base_raw[:, 0], ALU.add).then_inc(base_steps, 1)
            pool.wait_ge(x1_made, TILES)

            def biased(t, four, s):
                if not isinstance(t, int) or t >= 2:
                    pool.wait_ge(out_made, t - 1)
                pool.tensor_tensor(x1_bias[:, s % 2, :], x1[:, bass.ds(t, 1), :].rearrange("p t d -> p (t d)"),
                                   up_bias_sb[:], ALU.add).then_inc(bias_added, 1)

            walk1(pool, biased, 0)

        @block.scalar
        def _(act):
            def copy_chunk(q, s, use):
                act.wait_ge(chunk_made, q + 1)
                after(act, chunk_stored[s], use * 16)
                act.copy(chunk_out[:, s, :], chunk_ps[s][:]).then_inc(chunk_copied, 1)

            def sum_squares(t, p):
                after(act, rms_steps, (t - 2) * RMS_STEPS + 1 if not isinstance(t, int) or t >= 2 else 0)
                after(act, squared, t)
                act.activation(square[:], x1[:, bass.ds(t, 1), :].rearrange("p t d -> p (t d)"), ACT.Square,
                               scale=D ** -0.5, accum_out=sumsq[:, p:p + 1]).then_inc(squared, 1)

            copied = 0
            for n, (a, b) in enumerate(PIECES):
                for _ in range(2):
                    copy_chunk(copied, slot_of(copied), use_of(copied))
                    copied += 1
                act.wait_ge(up_in[n], 16)
                act.copy(up_hi[:, :, a:b], up_raw[:, :, a:b]).then_inc(up_hi_made, 1)
            while copied < EARLY:
                copy_chunk(copied, slot_of(copied), use_of(copied))
                copied += 1
            act.wait_ge(x_first, 16)
            sum_squares(0, 0)

            def step(t, pair, p, first, last):
                r = rms[:, p, 4:5]
                for half in range(2):
                    act.wait_ge(gate_ready, t * 2 + half + 1)
                    if half == 0:
                        act.wait_ge(rms_steps, (t + 1) * RMS_STEPS)
                    after(act, hid_made, t * 2 + half - 1)
                    act.activation(gelu[:, half, :], gate_ps[half][:], ACT.Gelu, scale=r).then_inc(gelu_done, 1)
                    if half == 0:
                        c = 0 if p == 0 else 2
                        copy_chunk(chunk(pair, c), c, chunk_use(pair, c))
                if not last:
                    if isinstance(t, int) and t == 1:
                        act.wait_ge(x_rest, 16)
                    sum_squares(t + 1, 1 - p)
                if not first:
                    copy_quant(t - 1)
                if p == 0:
                    copy_chunk(chunk(pair, 1), 1, chunk_use(pair, 1))

            def copy_quant(t):
                act.wait_ge(quant_turned, t + 1)
                after(act, y_ready, t)
                act.copy(quant_t[:], bank_t[:]).then_inc(quant_copied, 1)

            walk0(act, step)
            copy_quant(TILES - 1)
            act.wait_ge(small_in, 64)

            def step1(t, four, s):
                if live(t, 0):
                    act.wait_ge(x1_turned, t + 1)
                    after(act, down_ready, t - 1)
                    act.copy(x1_t[:, s % 2].rearrange("p k c -> p (k c)"), x1_t_ps[s % 2][:, 0:D]
                             ).then_inc(x1_copied, 1)
                if live(t, 1):
                    act.wait_ge(down_ready, t)
                    after(act, down_turned, t - 2)
                    act.copy(down_sb[:, (s + 1) % 2, :], down_ps[(s + 1) % 2][:, 0:P]).then_inc(down_copied, 1)
                if live(t, 2):
                    act.wait_ge(down_turned, t - 1)
                    after(act, up_ready, t - 3)
                    act.activation(down_relu[:, s % 2, :], turned_ps[s % 2][:, 0:P], ACT.Relu,
                                   bias=down_bias_sb[:]).then_inc(relu_done, 1)

            walk1(act, step1, 2)

        @block.vector
        def _(dve):
            def split(t, p):
                after(dve, xt_here[p], ((t - p) // 2 + 1) * 16 if isinstance(t, int) else 0)
                after(dve, h_split, t)
                dve.tensor_tensor(h_all[:].rearrange("p k (b l) -> p k b l", b=PER),
                                  xt_in[:, p].rearrange("p k (b l) -> p k b l", b=PER),
                                  scale_t[:, :, bass.ds(t * PER, PER)].unsqueeze(3).to_broadcast([P, K, PER, SEQ]),
                                  ALU.mult).then_inc(h_scaled, 1)
                dve.wait_ge(h_scaled, t + 1)
                after(dve, val_ready, 2 * (t - 1))
                dve.tensor_copy(h_hi[:, p], h_all[:]).then_inc(h_hi_made, 1)
                dve.wait_ge(h_hi_made, t + 1)
                dve.tensor_tensor(h_lo[:, p], h_all[:], h_hi[:, p].bitcast(F32), ALU.subtract).then_inc(h_split, 1)

            def gate(t, half):
                dve.wait_ge(gelu_done, t * 2 + half + 1)
                dve.wait_ge(val_ready, t * 2 + half + 1)
                after(dve, quant_made, t)
                dve.tensor_tensor(hid[:, half * HALF:(half + 1) * HALF], gelu[:, half, :], val_ps[half][:],
                                  ALU.mult).then_inc(hid_made, 1)

            def quantise(t, p):
                top, clipped, inverse, scale = (peak[:, p, n:n + 1] for n in range(4))
                r, done = rms[:, p, 4:5], t * PEAK_STEPS
                dve.wait_ge(hid_made, t * 2 + 2)
                dve.tensor_reduce(top, hid[:], AX.X, ALU.max, apply_absolute_value=True).then_inc(peak_steps, 1)
                dve.wait_ge(rms_steps, (t + 1) * RMS_STEPS)
                dve.wait_ge(peak_steps, done + 1)
                dve.tensor_scalar(clipped, top, r, TINY, ALU.mult, ALU.max).then_inc(peak_steps, 1)
                dve.wait_ge(peak_steps, done + 2)
                dve.reciprocal(inverse, clipped).then_inc(peak_steps, 1)
                dve.wait_ge(peak_steps, done + 3)
                dve.tensor_scalar(scale, inverse, r, QMAX, ALU.mult, ALU.mult).then_inc(peak_steps, 1)
                dve.wait_ge(peak_steps, done + 4)
                dve.tensor_scalar(hid[:], hid[:], scale, ROUND, ALU.mult, ALU.add).then_inc(hid_rounded, 1)
                dve.wait_ge(hid_rounded, t + 1)
                after(dve, quant_turned, t)
                dve.tensor_scalar(quant[:], hid[:], ROUND, QMAX, ALU.subtract, ALU.min).then_inc(quant_made, 1)

            def residual(t, p):
                dve.wait_ge(y_ready, t + 1)
                dve.tensor_scalar(factor[:, p:p + 1], peak[:, p, 1:2], weight_sum[:, 2:3], 1.0 / QMAX,
                                  ALU.mult, ALU.mult).then_inc(factor_made, 1)
                dve.wait_ge(factor_made, t + 1)
                tile = x1[:, bass.ds(t, 1), :].rearrange("p t d -> p (t d)")
                dve.scalar_tensor_tensor(out=tile, in0=y_ps, scalar=factor[:, p:p + 1], in1=tile,
                                         op0=ALU.mult, op1=ALU.add).then_inc(x1_made, 1)

            def quantise_weights():
                w = down_raw[:].rearrange("p c d -> p (c d)")
                dve.wait_ge(weights_total, 1)
                dve.tensor_scalar(weight_sum[:, 2:3], bank_y[:, 0:1], 1.0 / (D * FF), TINY, ALU.mult, ALU.max
                                  ).then_inc(weight_steps, 1)
                dve.wait_ge(weight_steps, 1)
                dve.reciprocal(weight_sum[:, 3:4], weight_sum[:, 2:3]).then_inc(weight_steps, 1)
                dve.wait_ge(weight_steps, 2)
                dve.tensor_scalar(w, w, weight_sum[:, 3:4], ROUND, ALU.mult, ALU.add).then_inc(weight_steps, 1)
                dve.wait_ge(weight_steps, 3)
                dve.tensor_scalar(w, w, ROUND, 1.0, ALU.subtract, ALU.min).then_inc(weight_steps, 1)
                dve.wait_ge(weight_steps, 4)
                dve.tensor_scalar(down_q[:].rearrange("p c d -> p (c d)"), w, -1.0, None, ALU.max
                                  ).then_inc(down_q_made, 1)

            dve.wait_ge(scale_ready, 1)
            dve.tensor_scalar(scale_t[:].rearrange("p k b -> p (k b)"), bank_y[:, 0:K * BATCH], 1.0, None, ALU.add
                              ).then_inc(scale_made, 1)
            dve.wait_ge(scale_made, 1)
            split(0, 0)
            for n, (a, b) in enumerate(PIECES):
                dve.wait_ge(up_hi_made, n + 1)
                dve.tensor_tensor(up_lo[:, :, a:b], up_raw[:, :, a:b], up_hi[:, :, a:b].bitcast(F32), ALU.subtract
                                  ).then_inc(up_lo_made, 1)

            def step(t, pair, p, first, last):
                gate(t, 0)
                if isinstance(t, int) and t == 1:
                    quantise_weights()
                if not last:
                    if not isinstance(t, int):
                        dve.wait_ge(xt_here[1 - p], (pair + 1 + p) * 16)
                    split(t + 1, 1 - p)
                gate(t, 1)
                quantise(t, p)
                if not first:
                    residual(t - 1, 1 - p)
                else:
                    dve.wait_ge(down_in, 16)
                    dve.tensor_reduce(weight_sum[:, 0:1], down_raw[:].rearrange("p c d -> p (c d)"), AX.X, ALU.add,
                                      apply_absolute_value=True).then_inc(weights_summed, 1)

            walk0(dve, step)
            residual(TILES - 1, 1)
            dve.wait_ge(base_steps, 2)

            def step1(t, four, s):
                if live(t, 0):
                    dve.wait_ge(delta_here[s], (four + 1) * 16)
                    after(dve, up_ready, t - 3)
                    dve.scalar_tensor_tensor(
                        out=w1[:, s].rearrange("p b k m c -> p b (k m c)"),
                        in0=delta_in[:, s].rearrange("p b k m c -> p b (k m c)"), scalar=DELTA,
                        in1=base[:].rearrange("p k m c -> p (k m c)").unsqueeze(1).to_broadcast([P, PER, K * 2 * P]),
                        op0=ALU.mult, op1=ALU.add).then_inc(w1_made, 1)
                if live(t, 3):
                    q = (s + 1) % 2
                    dve.wait_ge(up_ready, t - 2)
                    dve.wait_ge(bias_added, t - 2)
                    if isinstance(t, int):
                        after(dve, out_stored[q], (t - 3) // 2 * 16)
                    else:
                        dve.wait_ge(out_stored[q], (four * 2 + (s - 3) // 2) * 16)
                    dve.tensor_tensor(out_sb[:, q, :], up_ps[q][:, 0:D], x1_bias[:, q, :], ALU.add
                                      ).then_inc(out_made, 1)

            walk1(dve, step1, 3)

        @block.tensor
        def _(pe):
            def make_chunk(q, s, use):
                pe.wait_ge(chunk_here[s], (use + 1) * 16)
                after(pe, chunk_copied, q - (0, 2, 1)[s])
                pe.matmul(chunk_ps[s][:], cond2[:], chunk_in[:, s, :], start=True, stop=True).then_inc(chunk_made, 1)

            def up_project(t, p, half):
                pe.wait_ge(h_split, t + 1)
                for n, (bank, base_col, ready, used) in enumerate((
                        (gate_ps[half], FF + half * HALF, gate_ready, gelu_done),
                        (val_ps[half], half * HALF, val_ready, hid_made))):
                    if isinstance(t, int) and t == 0:
                        pe.wait_ge(up_lo_made, 2 * half + n + 1)
                    after(pe, used, t * 2 + half - 1)
                    cols = slice(base_col, base_col + HALF)
                    for k in range(K):
                        hi, lo = h_hi[:, p, k, :], h_lo[:, p, k, :]
                        pe.matmul(bank[:], lo, up_hi[:, k, cols], start=(k == 0), stop=False)
                        pe.matmul(bank[:], hi, up_lo[:, k, cols], start=False, stop=False)
                        last = pe.matmul(bank[:], hi, up_hi[:, k, cols], start=False, stop=(k == K - 1))
                    last.then_inc(ready, 1)

            def turn_quant(t):
                pe.wait_ge(quant_made, t + 1)
                after(pe, quant_copied, t)
                for c in range(FC):
                    last = pe.transpose(bank_t[:, c, :], quant[:, c * P:(c + 1) * P], ident_b[:])
                last.then_inc(quant_turned, 1)

            def down_project(t):
                pe.wait_ge(quant_copied, t + 1)
                after(pe, x1_made, t)
                for c in range(FC):
                    last = pe.matmul(y_ps, quant_t[:, c, :], down_q[:, c, :], start=(c == 0), stop=(c == FC - 1))
                last.then_inc(y_ready, 1)

            pe.wait_ge(cond_in, 32)
            pe.wait_ge(norm_in, 16)
            for k in range(K):
                last = pe.matmul(bank_y[:, k * BATCH:(k + 1) * BATCH], norm_sb[:, k * P:(k + 1) * P],
                                 cond2[0:C, 0:BATCH], start=True, stop=True)
            last.then_inc(scale_ready, 1)
            for q in range(EARLY):
                make_chunk(q, slot_of(q), use_of(q))

            def step(t, pair, p, first, last):
                up_project(t, p, 0)
                c = 0 if p == 0 else 2
                make_chunk(chunk(pair, c), c, chunk_use(pair, c))
                if isinstance(t, int) and t == 1:
                    pe.wait_ge(weights_summed, 1)
                    pe.wait_ge(scale_made, 1)
                    pe.wait_ge(ones_made, 1)
                    pe.matmul(bank_y[:, 0:1], ones[:], weight_sum[:, 0:1], start=True, stop=True
                              ).then_inc(weights_total, 1)
                    pe.wait_ge(identity_made, 1)
                up_project(t, p, 1)
                if not first:
                    turn_quant(t - 1)
                if p == 0:
                    make_chunk(chunk(pair, 1), 1, chunk_use(pair, 1))
                if not first:
                    if isinstance(t, int) and t == 1:
                        pe.wait_ge(down_q_made, 1)
                    down_project(t - 1)

            walk0(pe, step)
            turn_quant(TILES - 1)
            down_project(TILES - 1)
            pe.wait_ge(x1_made, TILES)
            pe.wait_ge(identf_made, 1)

            def step1(t, four, s):
                if live(t, 0):
                    pe.wait_ge(x1_here[s], (four + 1) * 16)
                    after(pe, x1_copied, t - 1)
                    for k in range(K):
                        last = pe.transpose(x1_t_ps[s % 2][:, k * P:(k + 1) * P],
                                            x1_tile[:, s, k * P:(k + 1) * P], ident[:])
                    last.then_inc(x1_turned, 1)
                if live(t, 1):
                    q, w = (s + 1) % 2, (s + RING - 1) % RING
                    pe.wait_ge(x1_copied, t)
                    pe.wait_ge(w1_made, t)
                    after(pe, down_copied, t - 2)
                    for b in range(PER):
                        rows = slice(b * SEQ, (b + 1) * SEQ)
                        for k in range(K):
                            last = pe.matmul(down_ps[q][rows, 0:BN], x1_t[:, q, k, rows], w1[:, w, b, k, 0, :],
                                             start=(k == 0), stop=(k == K - 1))
                    last.then_inc(down_ready, 1)
                if live(t, 2):
                    q = s % 2
                    pe.wait_ge(down_copied, t - 1)
                    after(pe, relu_done, t - 2)
                    pe.transpose(turned_ps[q][:, 0:P], down_sb[:, q, :], ident[:]).then_inc(down_turned, 1)
                if live(t, 3):
                    q, w = (s + 1) % 2, (s + RING - 3) % RING
                    pe.wait_ge(relu_done, t - 2)
                    after(pe, out_made, t - 4)
                    for b in range(PER):
                        rows = slice(b * SEQ, (b + 1) * SEQ)
                        last = pe.matmul(up_ps[q][rows, 0:D].rearrange("p (k c) -> p k c", k=K),
                                         down_relu[:, q, rows], w1[:, w, b, :, 1, :], start=True, stop=True)
                    last.then_inc(up_ready, 1)

            walk1(pe, step1, 3)


def layouts(np, x, cond, norm_w, up_w, down_w, wd, bd, wu, bu, wdd, bdd, wdu, bdu):
    n_chunk = CHUNKS // 2
    down_rows = lambda a, *rest: a.reshape(BN, K, P, *rest)
    up_rows = lambda a, *rest: a.reshape(K, P, BN, *rest)
    down_gen = wdd.reshape(BN, K, n_chunk, ROWS, C).transpose(2, 1, 4, 3, 0)
    up_gen = wdu.reshape(K, P, n_chunk, ROWS, C).transpose(2, 0, 4, 3, 1)
    both = lambda a, b: np.stack([down_rows(a).transpose(2, 1, 0), up_rows(b).transpose(2, 0, 1)], axis=2)
    return {
        "x": x.reshape(TILES, P, D),
        "x_t": x.reshape(TILES, P, K, P).transpose(0, 3, 2, 1),
        "cond_t": cond.T,
        "norm_t": norm_w.T,
        "up_t": up_w.reshape(2 * FF, K, P).transpose(2, 1, 0),
        "down_t": down_w.reshape(D, FC, P).transpose(2, 1, 0),
        "gen_w": np.concatenate([down_gen, up_gen]).reshape(CHUNKS, P, ROWS * P),
        "base_w": both(wd, wu),
        "base_b": both(bdd, bdu),
        "down_bias": bd.reshape(BN, 1),
        "up_bias": bu.reshape(1, D),
    }


def kernel(x, cond_256, L0_cond_norm_w, L0_cond_up_w, L0_cond_down_w, L1_cond_Wd, L1_cond_bd, L1_cond_Wu,
           L1_cond_bu, L1_cond_Wdd, L1_cond_bdd, L1_cond_Wdu, L1_cond_bdu):
    import numpy as np
    import concourse.bacc as bacc
    from concourse.bass_utils import run_bass_kernel_spmd

    given = [np.asarray(a) for a in (x, cond_256, L0_cond_norm_w, L0_cond_up_w, L0_cond_down_w, L1_cond_Wd,
                                     L1_cond_bd, L1_cond_Wu, L1_cond_bu, L1_cond_Wdd, L1_cond_bdd, L1_cond_Wdu,
                                     L1_cond_bdu)]
    arrays = {name: np.ascontiguousarray(a) for name, a in layouts(np, *given).items()}
    nc = bacc.Bacc("TRN2", target_bir_lowering=False, num_devices=1)
    args = {name: nc.dram_tensor(f"in_{name}", a.shape, mybir.dt.from_np(a.dtype), kind="ExternalInput").ap()
            for name, a in arrays.items()}
    out = nc.dram_tensor("out", [TILES, P, D], F32, kind="ExternalOutput").ap()
    build(nc, **args, out=out)
    r = run_bass_kernel_spmd(nc, [{f"in_{name}": a for name, a in arrays.items()}], core_ids=[0])
    return r.results[0]["out"].reshape(BATCH, SEQ, D)
```

```python
from contextlib import ExitStack

import concourse.bass as bass
from concourse import mybir
from concourse.alu_op_type import AluOpType as ALU

ACT = mybir.ActivationFunctionType
AX = mybir.AxisListType
F32 = mybir.dt.float32
F32R = mybir.dt.float32r
BF16 = mybir.dt.bfloat16

P = 128
BATCH, SEQ, D, C = 64, 64, 256, 64
FF, BN = 1024, 128
TILES = BATCH * SEQ // P
K = D // P
PER = P // SEQ
FC = FF // P
HALF = FF // 2
ROWS = 4
CHUNKS = 2 * BN // ROWS
SLOTS = 4
MAKERS = CHUNKS // SLOTS
PAIRS = TILES // 2
RING = 8
WRING = 4
ROUND = 12582912.0
QMAX = 127.0
DELTA = 0.1
EPS = 1e-6
TINY = 1e-5
assert MAKERS % 2 == 0 and PAIRS - MAKERS // 2 == RING


def after(engine, semaphore, value):
    if not isinstance(value, int) or value > 0:
        engine.wait_ge(semaphore, value)


def build(nc, x, x_t, cond_t, norm_t, up_t, down_t, gen_w, base_w, base_b, down_bias, up_bias, out):
    scratch = nc.dram_tensor("layer1_weights", [BATCH, K, 2 * P, P], F32, kind="Internal").ap()

    with ExitStack() as ctx:
        def sb(name, shape, dt=F32):
            return ctx.enter_context(nc.sbuf_tensor(name, shape, dt))

        def sem(name):
            return ctx.enter_context(nc.semaphore(name))

        x1 = sb("x1", [P, TILES, D])
        up_hi = sb("up_hi", [P, K, 2 * FF], F32R)
        up_lo = sb("up_lo", [P, K, 2 * FF], F32R)
        down_q = sb("down_q", [P, FC, D], BF16)
        norm_sb = sb("norm_sb", [C, D])
        scale_t = sb("scale_t", [P, K, BATCH])
        xt_in = sb("xt_in", [P, 2, K, P])
        h_all = sb("h_all", [P, K, P])
        h_hi = sb("h_hi", [P, 2, K, P], F32R)
        h_lo = sb("h_lo", [P, 2, K, P], F32R)
        gelu = sb("gelu", [P, 2, HALF])
        hid = sb("hid", [P, FF])
        quant = sb("quant", [P, FF], BF16)
        quant_t = sb("quant_t", [P, FC, P], BF16)
        square = sb("square", [P, D])
        meansq = sb("meansq", [P, 2])
        rms = sb("rms", [P, 2, 5])
        peak = sb("peak", [P, 2, 4])
        factor = sb("factor", [P, 2])
        numbers = sb("numbers", [P, 3])
        weight_sum = sb("weight_sum", [P, 4])
        ident_b = sb("ident_b", [P, P], BF16)
        ident = sb("ident", [P, P])
        ones = sb("ones", [P, P])
        cond2 = sb("cond2", [P, P])
        cond2_hi = sb("cond2_hi", [P, P], F32R)
        cond2_lo = sb("cond2_lo", [P, P], F32R)
        chunk_in = sb("chunk_in", [P, SLOTS, ROWS * P])
        chunk_hi = sb("chunk_hi", [P, SLOTS, ROWS * P], F32R)
        chunk_lo = sb("chunk_lo", [P, SLOTS, ROWS * P], F32R)
        chunk_out = sb("chunk_out", [P, SLOTS, ROWS * P])
        base = sb("base", [P, K, 2, P])
        base_raw = sb("base_raw", [P, 2, K, 2, P])
        w1 = sb("w1", [P, WRING, PER, K, 2, P])
        x1_tile = sb("x1_tile", [P, RING, D])
        x1_t = sb("x1_t", [P, 2, K, P])
        down_sb = sb("down_sb", [P, 2, P])
        down_relu = sb("down_relu", [P, 2, P])
        x1_bias = sb("x1_bias", [P, 2, D])
        out_sb = sb("out_sb", [P, 2, D])
        down_bias_sb = sb("down_bias_sb", [P, 1])
        up_bias_sb = sb("up_bias_sb", [P, D])

        with ExitStack() as start:
            up_raw = start.enter_context(nc.sbuf_tensor("up_raw", [P, K, 2 * FF], F32))
            down_raw = start.enter_context(nc.sbuf_tensor("down_raw", [P, FC, D], F32))
            down_size = start.enter_context(nc.sbuf_tensor("down_size", [P, FC, D], BF16))
        delta_in = sb("delta_in", [P, RING, PER, K, 2, P])

        banks = [ctx.enter_context(nc.psum_tensor(f"bank{i}", [P, HALF], F32)) for i in range(4)]
        bank_t = ctx.enter_context(nc.psum_tensor("bank_t", [P, FC, P], BF16))
        bank_y = ctx.enter_context(nc.psum_tensor("bank_y", [P, HALF], F32))
        bank_g = [ctx.enter_context(nc.psum_tensor(f"bank_g{i}", [P, HALF], F32)) for i in range(2)]
        gate_ps, val_ps = [banks[0], banks[2]], [banks[1], banks[3]]
        y_ps = bank_y[:, 0:D]
        x1_t_ps = [banks[0], banks[1]]
        down_ps = [banks[2], banks[3]]
        turned_ps = [bank_y, bank_y]
        up_ps = [bank_g[0], bank_g[1]]

        cond_in, norm_in, down_in = sem("cond_in"), sem("norm_in"), sem("down_in")
        up_in = [sem(f"up_in{n}") for n in range(4)]
        small_in = sem("small_in")
        x_here = [sem(f"x_here{p}") for p in range(2)]
        xt_here = [sem(f"xt_here{p}") for p in range(2)]
        cleared, identity_made, ones_made = sem("cleared"), sem("identity_made"), sem("ones_made")
        identf_made, numbers_made = sem("identf_made"), sem("numbers_made")
        scale_ready, scale_made = sem("scale_ready"), sem("scale_made")
        cond_hi_made, cond_split = sem("cond_hi_made"), sem("cond_split")
        up_hi_made, up_lo_made = sem("up_hi_made"), sem("up_lo_made")
        weights_summed, weights_total = sem("weights_summed"), sem("weights_total")
        weight_steps, down_q_made = sem("weight_steps"), sem("down_q_made")
        base_steps = sem("base_steps")
        chunk_here = [sem(f"chunk_here{s}") for s in range(SLOTS)]
        chunk_stored = [sem(f"chunk_stored{s}") for s in range(SLOTS)]
        chunk_hi_made, chunk_split = sem("chunk_hi_made"), sem("chunk_split")
        chunk_made, chunk_copied = sem("chunk_made"), sem("chunk_copied")
        h_scaled, h_hi_made, h_split = sem("h_scaled"), sem("h_hi_made"), sem("h_split")
        gate_ready, val_ready = sem("gate_ready"), sem("val_ready")
        squared, rms_steps = sem("squared"), sem("rms_steps")
        gelu_done, hid_made, peak_steps = sem("gelu_done"), sem("hid_made"), sem("peak_steps")
        hid_rounded, quant_made = sem("hid_rounded"), sem("quant_made")
        quant_turned, quant_copied = sem("quant_turned"), sem("quant_copied")
        y_ready, factor_made, x1_made = sem("y_ready"), sem("factor_made"), sem("x1_made")
        delta_first = sem("delta_first")
        delta_here = [sem(f"delta_here{s}") for s in range(RING)]
        x1_here = [sem(f"x1_here{s}") for s in range(RING)]
        w1_made, x1_turned, x1_copied = sem("w1_made"), sem("x1_turned"), sem("x1_copied")
        down_ready, down_copied = sem("down_ready"), sem("down_copied")
        down_turned, relu_done = sem("down_turned"), sem("relu_done")
        up_ready, bias_added, out_made = sem("up_ready"), sem("bias_added"), sem("out_made")
        out_stored = [sem(f"out_stored{p}") for p in range(2)]

        RMS_STEPS, PEAK_STEPS = 7, 4
        PIECES = [(FF + 0, FF + HALF), (0, HALF), (FF + HALF, 2 * FF), (HALF, FF)]
        block = ctx.enter_context(nc.Block())

        def walk0(engine, step):
            def pair_of_tiles(pair, makes):
                for p in range(2):
                    t = pair * 2 + p
                    splits = makes and not (isinstance(t, int) and t == MAKERS - 1)
                    step(t, pair, p, makes, splits)

            pair_of_tiles(0, True)
            with engine.Fori(1, MAKERS // 2 - 1) as pair:
                pair_of_tiles(pair, True)
            pair_of_tiles(MAKERS // 2 - 1, True)
            with engine.Fori(MAKERS // 2, PAIRS - 1) as pair:
                pair_of_tiles(pair, False)
            pair_of_tiles(PAIRS - 1, False)

        def walk1(engine, step, lag, done=0):
            for t in range(done, RING):
                step(t, 0, t)
            with engine.Fori(1, TILES // RING - 1) as eight:
                for s in range(RING):
                    step(eight * RING + s, eight, s)
            for t in range(TILES - RING, TILES + lag):
                step(t, t // RING, t % RING)

        def live(t, back):
            return not isinstance(t, int) or 0 <= t - back < TILES

        def is_tile(t, which):
            return isinstance(t, int) and t == which

        @block.sync
        def _(sp):
            def load_chunk(t, c):
                sp.dma_start(chunk_in[:, c, :], gen_w[t * SLOTS + c]).then_inc(chunk_here[c], 16)

            def store_chunk(t, c):
                q = t * SLOTS + c
                sp.wait_ge(chunk_copied, q + 1)
                target = scratch[:, :, bass.ds(q * ROWS, ROWS), :].rearrange("b k r c -> k b (r c)")
                sp.dma_start(target, chunk_out[:, c, :]).then_inc(chunk_stored[c], 16)

            def load_x(t, p):
                after(sp, h_split, t - 1)
                after(sp, squared, t - 1)
                sp.dma_start(xt_in[:, p], x_t[t]).then_inc(xt_here[p], 16)
                sp.dma_start(x1[:, bass.ds(t, 1), :].rearrange("p t d -> p (t d)"), x[t]).then_inc(x_here[p], 16)

            def load_up(n):
                a, b = PIECES[n]
                sp.dma_start(up_raw[:, :, a:b], up_t[:, :, a:b]).then_inc(up_in[n], 16)

            load_chunk(0, 0)
            sp.dma_start(norm_sb[:], norm_t).then_inc(norm_in, 16)
            load_up(0)
            sp.wait_ge(cleared, 1)
            for k in range(K):
                sp.dma_start(cond2[k * C:(k + 1) * C, k * BATCH:(k + 1) * BATCH], cond_t).then_inc(cond_in, 16)
            load_x(0, 0)
            load_chunk(0, 1)
            load_up(1)
            load_chunk(0, 2)
            load_chunk(0, 3)
            load_up(2)
            load_up(3)
            sp.dma_start(down_raw[:], down_t).then_inc(down_in, 16)
            load_x(1, 1)
            for c in range(SLOTS):
                sp.wait_ge(chunk_split, c + 1)
                load_chunk(1, c)

            def step(t, pair, p, makes, splits):
                if makes:
                    for c in range(SLOTS):
                        store_chunk(t, c)
                        if splits and not is_tile(t, MAKERS - 2):
                            sp.wait_ge(chunk_split, (t + 1) * SLOTS + c + 1)
                            load_chunk(t + 2, c)
                        if c == 1 and not is_tile(t, TILES - 2) and not is_tile(t, TILES - 1):
                            load_x(t + 2, p)
                else:
                    if not is_tile(t, TILES - 2) and not is_tile(t, TILES - 1):
                        load_x(t + 2, p)
                    if is_tile(t, MAKERS):
                        return
                    if p == 1:
                        sp.dma_start(delta_in[:, bass.ds(pair - MAKERS // 2, 1)]
                                     .rearrange("p t b k m c -> p (t b k m) c"),
                                     delta_of(pair - MAKERS // 2)).then_inc(delta_first, 16)

            def delta_of(t):
                return scratch[bass.ds(t * PER, PER)].rearrange("b k (m r) c -> r (b k m) c", m=2)

            def walk0_sync(step):
                def pair_of_tiles(pair, makes):
                    for p in range(2):
                        t = pair * 2 + p
                        step(t, pair, p, makes, makes and not is_tile(t, MAKERS - 1))

                pair_of_tiles(0, True)
                with sp.Fori(1, MAKERS // 2 - 1) as pair:
                    pair_of_tiles(pair, True)
                pair_of_tiles(MAKERS // 2 - 1, True)
                for c in range(SLOTS):
                    sp.wait_ge(chunk_stored[c], 16 * MAKERS)
                with sp.Fori(MAKERS // 2, PAIRS - 1) as pair:
                    pair_of_tiles(pair, False)
                pair_of_tiles(PAIRS - 1, False)

            walk0_sync(step)
            for target, source in ((base_raw[:, 0], base_w), (base_raw[:, 1], base_b),
                                   (down_bias_sb[:], down_bias), (up_bias_sb[:], up_bias.to_broadcast([P, D]))):
                sp.dma_start(target, source).then_inc(small_in, 16)

            def copy_x1(t, s):
                sp.wait_ge(x1_made, t + 1)
                sp.dma_start(x1_tile[:, s, :], x1[:, bass.ds(t, 1), :].rearrange("p t d -> p (t d)")
                             ).then_inc(x1_here[s], 16)

            for t in range(RING):
                copy_x1(t, t)

            def step1(t, eight, s):
                if not isinstance(t, int) or t + RING < TILES:
                    sp.wait_ge(w1_made, t + 1)
                    sp.wait_ge(x1_turned, t + 1)
                    sp.dma_start(delta_in[:, s].rearrange("p b k m c -> p (b k m) c"), delta_of(t + RING)
                                 ).then_inc(delta_here[s], 16)
                    copy_x1(t + RING, s)
                if live(t, 3):
                    sp.wait_ge(out_made, t - 2)
                    q = (s + 1) % 2
                    sp.dma_start(out[t - 3], out_sb[:, q, :]).then_inc(out_stored[q], 16)

            walk1(sp, step1, 3)
            for p in range(2):
                sp.wait_ge(out_stored[p], 16 * TILES // 2)

        @block.gpsimd
        def _(pool):
            pool.memset(cond2[:], 0.0).then_inc(cleared, 1)
            pool.memset(ident[:], 0.0).then_inc(cleared, 1)
            minus_half, eps, one_half = (numbers[:, n:n + 1] for n in range(3))
            for place, value in ((minus_half, -0.5), (eps, EPS), (one_half, 1.5)):
                pool.memset(place, value).then_inc(numbers_made, 1)
            pool.memset(ones[:], 1.0).then_inc(ones_made, 1)
            pool.wait_ge(cleared, 2)
            pool.affine_select(out=ident[:], in_=ident[:], compare_op=ALU.not_equal, fill=1.0, base=0,
                               pattern=[[-1, P]], channel_multiplier=1).then_inc(identf_made, 1)
            pool.wait_ge(identf_made, 1)
            pool.tensor_copy(ident_b[:], ident[:]).then_inc(identity_made, 1)
            pool.wait_ge(numbers_made, 3)

            def root(t, pair, p, makes, splits):
                v, guess, sq, fix, r = (rms[:, p, n:n + 1] for n in range(5))
                done = t * RMS_STEPS
                pool.wait_ge(squared, t + 1)
                after(pool, peak_steps, (t - 1) * PEAK_STEPS)
                for n, (result, one, other, op) in enumerate((
                        (v, meansq[:, p:p + 1], eps, ALU.add), (guess, v, minus_half, ALU.pow),
                        (sq, guess, guess, ALU.mult), (sq, sq, v, ALU.mult), (fix, sq, minus_half, ALU.mult),
                        (fix, fix, one_half, ALU.add), (r, guess, fix, ALU.mult))):
                    if n:
                        pool.wait_ge(rms_steps, done + n)
                    pool.tensor_tensor(result, one, other, op).then_inc(rms_steps, 1)

            walk0(pool, root)

            pool.wait_ge(small_in, 64)
            pool.tensor_scalar(base[:], base_raw[:, 1], DELTA, None, ALU.mult).then_inc(base_steps, 1)
            pool.wait_ge(base_steps, 1)
            pool.tensor_tensor(base[:], base[:], base_raw[:, 0], ALU.add).then_inc(base_steps, 1)

            def biased(t, eight, s):
                pool.wait_ge(x1_made, t + 1)
                after(pool, out_made, t - 1)
                pool.tensor_tensor(x1_bias[:, s % 2, :], x1[:, bass.ds(t, 1), :].rearrange("p t d -> p (t d)"),
                                   up_bias_sb[:], ALU.add).then_inc(bias_added, 1)

            walk1(pool, biased, 0)

        @block.scalar
        def _(act):
            def high_chunk(t, c):
                q = t * SLOTS + c
                act.wait_ge(chunk_here[c], (t + 1) * 16)
                after(act, chunk_made, q - SLOTS + 1)
                act.copy(chunk_hi[:, c, :], chunk_in[:, c, :]).then_inc(chunk_hi_made, 1)

            def copy_chunk(t, c):
                act.wait_ge(chunk_made, t * SLOTS + c + 1)
                after(act, chunk_stored[c], t * 16)
                act.copy(chunk_out[:, c, :], bank_g[c % 2][:]).then_inc(chunk_copied, 1)

            def mean_squares(t, pair, p):
                act.wait_ge(x_here[p], (pair + 1) * 16)
                after(act, rms_steps, (t - 2) * RMS_STEPS + 1)
                after(act, squared, t)
                act.activation(square[:], x1[:, bass.ds(t, 1), :].rearrange("p t d -> p (t d)"), ACT.Square,
                               scale=D ** -0.5, accum_out=meansq[:, p:p + 1]).then_inc(squared, 1)

            def copy_quant(t):
                act.wait_ge(quant_turned, t + 1)
                after(act, y_ready, t)
                for n in range(2):
                    blocks = slice(n * FC // 2, (n + 1) * FC // 2)
                    act.copy(quant_t[:, blocks, :], bank_t[:, blocks, :]).then_inc(quant_copied, 1)

            def high_up(n):
                a, b = PIECES[n]
                act.wait_ge(up_in[n], 16)
                act.copy(up_hi[:, :, a:b], up_raw[:, :, a:b]).then_inc(up_hi_made, 1)

            act.wait_ge(cond_in, 32)
            act.copy(cond2_hi[:], cond2[:]).then_inc(cond_hi_made, 1)
            high_chunk(0, 0)
            high_up(0)
            high_chunk(0, 1)
            high_up(1)
            high_chunk(0, 2)
            high_chunk(0, 3)
            mean_squares(0, 0, 0)

            def step(t, pair, p, makes, splits):
                if is_tile(t, 0):
                    for c in range(SLOTS):
                        copy_chunk(t, c)
                        if c == 1:
                            high_up(2)
                    high_up(3)
                    for c in range(SLOTS):
                        high_chunk(t + 1, c)
                r = rms[:, p, 4:5]
                for half in range(2):
                    act.wait_ge(gate_ready, t * 2 + half + 1)
                    if half == 0:
                        act.wait_ge(rms_steps, (t + 1) * RMS_STEPS)
                    after(act, hid_made, t * 2 + half - 1)
                    act.activation(gelu[:, half, :], gate_ps[half][:], ACT.Gelu, scale=r).then_inc(gelu_done, 1)
                    if half == 0 and makes and not is_tile(t, 0):
                        for c in range(2):
                            copy_chunk(t, c)
                        if splits:
                            for c in range(2):
                                high_chunk(t + 1, c)
                if is_tile(t, 0):
                    act.wait_ge(down_in, 16)
                    act.activation(down_size[:], down_raw[:], ACT.Abs, accum_out=weight_sum[:, 0:1]
                                   ).then_inc(weights_summed, 1)
                if not is_tile(t, TILES - 1):
                    mean_squares(t + 1, pair + p, 1 - p)
                if not is_tile(t, 0):
                    copy_quant(t - 1)
                    if makes:
                        for c in range(2, SLOTS):
                            copy_chunk(t, c)
                        if splits:
                            for c in range(2, SLOTS):
                                high_chunk(t + 1, c)

            def step1(t, eight, s):
                if live(t, 0):
                    act.wait_ge(x1_turned, t + 1)
                    after(act, down_ready, t - 1)
                    act.copy(x1_t[:, s % 2].rearrange("p k c -> p (k c)"), x1_t_ps[s % 2][:, 0:D]
                             ).then_inc(x1_copied, 1)
                if live(t, 1):
                    act.wait_ge(down_ready, t)
                    after(act, down_turned, t - 2)
                    act.copy(down_sb[:, (s + 1) % 2, :], down_ps[(s + 1) % 2][:, 0:P]).then_inc(down_copied, 1)
                if live(t, 2):
                    act.wait_ge(down_turned, t - 1)
                    after(act, up_ready, t - 3)
                    act.activation(down_relu[:, s % 2, :], turned_ps[s % 2][:, 0:P], ACT.Relu,
                                   bias=down_bias_sb[:]).then_inc(relu_done, 1)

            walk0(act, step)
            act.wait_ge(small_in, 64)
            step1(0, 0, 0)
            copy_quant(TILES - 1)
            walk1(act, step1, 2, done=1)

        @block.vector
        def _(dve):
            def split(t, pair, p):
                dve.wait_ge(xt_here[p], (pair + 1) * 16)
                after(dve, h_split, t)
                dve.tensor_tensor(h_all[:].rearrange("p k (b l) -> p k b l", b=PER),
                                  xt_in[:, p].rearrange("p k (b l) -> p k b l", b=PER),
                                  scale_t[:, :, bass.ds(t * PER, PER)].unsqueeze(3).to_broadcast([P, K, PER, SEQ]),
                                  ALU.mult).then_inc(h_scaled, 1)
                dve.wait_ge(h_scaled, t + 1)
                after(dve, val_ready, 2 * (t - 1))
                dve.tensor_copy(h_hi[:, p], h_all[:]).then_inc(h_hi_made, 1)
                dve.wait_ge(h_hi_made, t + 1)
                dve.tensor_tensor(h_lo[:, p], h_all[:], h_hi[:, p].bitcast(F32), ALU.subtract).then_inc(h_split, 1)

            def split_chunk(t, c):
                q = t * SLOTS + c
                dve.wait_ge(chunk_hi_made, q + 1)
                dve.tensor_tensor(chunk_lo[:, c, :], chunk_in[:, c, :], chunk_hi[:, c, :].bitcast(F32),
                                  ALU.subtract).then_inc(chunk_split, 1)

            def split_up(n):
                a, b = PIECES[n]
                dve.wait_ge(up_hi_made, n + 1)
                dve.tensor_tensor(up_lo[:, :, a:b], up_raw[:, :, a:b], up_hi[:, :, a:b].bitcast(F32), ALU.subtract
                                  ).then_inc(up_lo_made, 1)

            def gate(t, half):
                dve.wait_ge(gelu_done, t * 2 + half + 1)
                dve.wait_ge(val_ready, t * 2 + half + 1)
                after(dve, quant_made, t)
                dve.tensor_tensor(hid[:, half * HALF:(half + 1) * HALF], gelu[:, half, :], val_ps[half][:],
                                  ALU.mult).then_inc(hid_made, 1)

            def quantise(t, p):
                top, clipped, inverse, scale = (peak[:, p, n:n + 1] for n in range(4))
                r, done = rms[:, p, 4:5], t * PEAK_STEPS
                dve.wait_ge(hid_made, t * 2 + 2)
                dve.tensor_reduce(top, hid[:], AX.X, ALU.max, apply_absolute_value=True).then_inc(peak_steps, 1)
                dve.wait_ge(rms_steps, (t + 1) * RMS_STEPS)
                dve.wait_ge(peak_steps, done + 1)
                dve.tensor_scalar(clipped, top, r, TINY, ALU.mult, ALU.max).then_inc(peak_steps, 1)
                dve.wait_ge(peak_steps, done + 2)
                dve.reciprocal(inverse, clipped).then_inc(peak_steps, 1)
                dve.wait_ge(peak_steps, done + 3)
                dve.tensor_scalar(scale, inverse, r, QMAX, ALU.mult, ALU.mult).then_inc(peak_steps, 1)
                dve.wait_ge(peak_steps, done + 4)
                dve.tensor_scalar(hid[:], hid[:], scale, ROUND, ALU.mult, ALU.add).then_inc(hid_rounded, 1)
                dve.wait_ge(hid_rounded, t + 1)
                after(dve, quant_turned, t)
                dve.tensor_scalar(quant[:], hid[:], ROUND, QMAX, ALU.subtract, ALU.min).then_inc(quant_made, 1)

            def residual(t, p):
                dve.wait_ge(y_ready, t + 1)
                dve.tensor_scalar(factor[:, p:p + 1], peak[:, p, 1:2], weight_sum[:, 2:3], 1.0 / QMAX,
                                  ALU.mult, ALU.mult).then_inc(factor_made, 1)
                dve.wait_ge(factor_made, t + 1)
                tile = x1[:, bass.ds(t, 1), :].rearrange("p t d -> p (t d)")
                dve.scalar_tensor_tensor(out=tile, in0=y_ps, scalar=factor[:, p:p + 1], in1=tile,
                                         op0=ALU.mult, op1=ALU.add).then_inc(x1_made, 1)

            def quantise_weights():
                w = down_raw[:].rearrange("p c d -> p (c d)")
                dve.wait_ge(weights_total, 1)
                dve.tensor_scalar(weight_sum[:, 2:3], bank_y[:, 0:1], 1.0 / (D * FF), TINY, ALU.mult, ALU.max
                                  ).then_inc(weight_steps, 1)
                dve.wait_ge(weight_steps, 1)
                dve.reciprocal(weight_sum[:, 3:4], weight_sum[:, 2:3]).then_inc(weight_steps, 1)
                dve.wait_ge(weight_steps, 2)
                dve.tensor_scalar(w, w, weight_sum[:, 3:4], ROUND, ALU.mult, ALU.add).then_inc(weight_steps, 1)
                dve.wait_ge(weight_steps, 3)
                dve.tensor_scalar(w, w, ROUND, 1.0, ALU.subtract, ALU.min).then_inc(weight_steps, 1)
                dve.wait_ge(weight_steps, 4)
                dve.tensor_scalar(down_q[:].rearrange("p c d -> p (c d)"), w, -1.0, None, ALU.max
                                  ).then_inc(down_q_made, 1)

            dve.wait_ge(cond_hi_made, 1)
            dve.tensor_tensor(cond2_lo[:], cond2[:], cond2_hi[:].bitcast(F32), ALU.subtract).then_inc(cond_split, 1)
            split_chunk(0, 0)
            dve.wait_ge(scale_ready, 1)
            dve.tensor_scalar(scale_t[:].rearrange("p k b -> p (k b)"), bank_y[:, 0:K * BATCH], 1.0, None, ALU.add
                              ).then_inc(scale_made, 1)
            dve.wait_ge(scale_made, 1)
            split(0, 0, 0)
            split_up(0)
            split_chunk(0, 1)
            split_up(1)
            split_chunk(0, 2)
            split_chunk(0, 3)
            split_up(2)
            split_up(3)

            def step(t, pair, p, makes, splits):
                if is_tile(t, 0):
                    split_chunk(t + 1, 0)
                    split_chunk(t + 1, 1)
                gate(t, 0)
                if not is_tile(t, TILES - 1):
                    split(t + 1, pair + p, 1 - p)
                gate(t, 1)
                if splits and not is_tile(t, 0):
                    split_chunk(t + 1, 0)
                    split_chunk(t + 1, 1)
                quantise(t, p)
                if is_tile(t, 0):
                    quantise_weights()
                else:
                    residual(t - 1, 1 - p)
                if splits:
                    split_chunk(t + 1, 2)
                    split_chunk(t + 1, 3)

            def step1(t, eight, s):
                if live(t, 0):
                    if isinstance(t, int) and t < RING:
                        dve.wait_ge(delta_first, 16 * RING)
                    else:
                        dve.wait_ge(delta_here[s], eight * 16)
                    after(dve, up_ready, t - WRING + 1)
                    dve.scalar_tensor_tensor(
                        out=w1[:, s % WRING].rearrange("p b k m c -> p b (k m c)"),
                        in0=delta_in[:, s].rearrange("p b k m c -> p b (k m c)"), scalar=DELTA,
                        in1=base[:].rearrange("p k m c -> p (k m c)").unsqueeze(1).to_broadcast([P, PER, K * 2 * P]),
                        op0=ALU.mult, op1=ALU.add).then_inc(w1_made, 1)
                if live(t, 3):
                    q = (s + 1) % 2
                    dve.wait_ge(up_ready, t - 2)
                    dve.wait_ge(bias_added, t - 2)
                    after(dve, out_stored[q], (eight * (RING // 2) + (s - 3) // 2) * 16)
                    dve.tensor_tensor(out_sb[:, q, :], up_ps[q][:, 0:D], x1_bias[:, q, :], ALU.add
                                      ).then_inc(out_made, 1)

            walk0(dve, step)
            dve.wait_ge(base_steps, 2)
            for t in range(2):
                step1(t, 0, t)
            residual(TILES - 1, 1)
            walk1(dve, step1, 3, done=2)

        @block.tensor
        def _(pe):
            def make_chunk(t, c):
                q = t * SLOTS + c
                pe.wait_ge(chunk_split, q + 1)
                after(pe, chunk_copied, q - 1)
                product = bank_g[c % 2][:]
                pe.matmul(product, cond2_lo[:], chunk_hi[:, c, :], start=True, stop=False)
                pe.matmul(product, cond2_hi[:], chunk_lo[:, c, :], start=False, stop=False)
                pe.matmul(product, cond2_hi[:], chunk_hi[:, c, :], start=False, stop=True).then_inc(chunk_made, 1)

            def up_project(t, p, half):
                pe.wait_ge(h_split, t + 1)
                for n, (bank, first_col, ready, used) in enumerate((
                        (gate_ps[half], FF + half * HALF, gate_ready, gelu_done),
                        (val_ps[half], half * HALF, val_ready, hid_made))):
                    if is_tile(t, 0):
                        pe.wait_ge(up_lo_made, 2 * half + n + 1)
                    after(pe, used, t * 2 + half - 1)
                    cols = slice(first_col, first_col + HALF)
                    for k in range(K):
                        hi, lo = h_hi[:, p, k, :], h_lo[:, p, k, :]
                        pe.matmul(bank[:], lo, up_hi[:, k, cols], start=(k == 0), stop=False)
                        pe.matmul(bank[:], hi, up_lo[:, k, cols], start=False, stop=False)
                        last = pe.matmul(bank[:], hi, up_hi[:, k, cols], start=False, stop=(k == K - 1))
                    last.then_inc(ready, 1)

            def turn_quant(t):
                pe.wait_ge(quant_made, t + 1)
                after(pe, quant_copied, t * 2)
                for c in range(FC):
                    last = pe.transpose(bank_t[:, c, :], quant[:, c * P:(c + 1) * P], ident_b[:])
                last.then_inc(quant_turned, 1)

            def down_project(t):
                after(pe, x1_made, t)
                for c in range(FC):
                    if c % (FC // 2) == 0:
                        pe.wait_ge(quant_copied, t * 2 + 1 + c // (FC // 2))
                    last = pe.matmul(y_ps, quant_t[:, c, :], down_q[:, c, :], start=(c == 0), stop=(c == FC - 1))
                last.then_inc(y_ready, 1)

            pe.wait_ge(cond_in, 32)
            pe.wait_ge(norm_in, 16)
            for k in range(K):
                last = pe.matmul(bank_y[:, k * BATCH:(k + 1) * BATCH], norm_sb[:, k * P:(k + 1) * P],
                                 cond2[0:C, 0:BATCH], start=True, stop=True)
            last.then_inc(scale_ready, 1)
            pe.wait_ge(cond_split, 1)
            for c in range(SLOTS):
                make_chunk(0, c)

            def step(t, pair, p, makes, splits):
                up_project(t, p, 0)
                if makes and not is_tile(t, 0):
                    make_chunk(t, 0)
                    make_chunk(t, 1)
                up_project(t, p, 1)
                if is_tile(t, 0):
                    pe.wait_ge(weights_summed, 1)
                    pe.wait_ge(scale_made, 1)
                    pe.wait_ge(ones_made, 1)
                    pe.matmul(bank_y[:, 0:1], ones[:], weight_sum[:, 0:1], start=True, stop=True
                              ).then_inc(weights_total, 1)
                    pe.wait_ge(identity_made, 1)
                    return
                turn_quant(t - 1)
                if makes:
                    make_chunk(t, 2)
                    make_chunk(t, 3)
                if is_tile(t, 1):
                    pe.wait_ge(down_q_made, 1)
                down_project(t - 1)

            def step1(t, eight, s):
                if live(t, 0):
                    pe.wait_ge(x1_here[s], (eight + 1) * 16)
                    after(pe, x1_copied, t - 1)
                    for k in range(K):
                        last = pe.transpose(x1_t_ps[s % 2][:, k * P:(k + 1) * P],
                                            x1_tile[:, s, k * P:(k + 1) * P], ident[:])
                    last.then_inc(x1_turned, 1)
                if live(t, 1):
                    q, w = (s + 1) % 2, (s + WRING - 1) % WRING
                    pe.wait_ge(x1_copied, t)
                    pe.wait_ge(w1_made, t)
                    after(pe, down_copied, t - 2)
                    for b in range(PER):
                        rows = slice(b * SEQ, (b + 1) * SEQ)
                        for k in range(K):
                            last = pe.matmul(down_ps[q][rows, 0:BN], x1_t[:, q, k, rows], w1[:, w, b, k, 0, :],
                                             start=(k == 0), stop=(k == K - 1))
                    last.then_inc(down_ready, 1)
                if live(t, 2):
                    q = s % 2
                    pe.wait_ge(down_copied, t - 1)
                    after(pe, relu_done, t - 2)
                    pe.transpose(turned_ps[q][:, 0:P], down_sb[:, q, :], ident[:]).then_inc(down_turned, 1)
                if live(t, 3):
                    q, w = (s + 1) % 2, (s + WRING - 3) % WRING
                    pe.wait_ge(relu_done, t - 2)
                    after(pe, out_made, t - 4)
                    for b in range(PER):
                        rows = slice(b * SEQ, (b + 1) * SEQ)
                        last = pe.matmul(up_ps[q][rows, 0:D].rearrange("p (k c) -> p k c", k=K),
                                         down_relu[:, q, rows], w1[:, w, b, :, 1, :], start=True, stop=True)
                    last.then_inc(up_ready, 1)

            walk0(pe, step)
            pe.wait_ge(hid_made, 2 * TILES)
            pe.wait_ge(identf_made, 1)
            step1(0, 0, 0)
            turn_quant(TILES - 1)
            step1(1, 0, 1)
            down_project(TILES - 1)
            pe.wait_ge(x1_made, TILES)
            walk1(pe, step1, 3, done=2)


def layouts(np, x, cond, norm_w, up_w, down_w, wd, bd, wu, bu, wdd, bdd, wdu, bdu):
    n_chunk = CHUNKS // 2
    down_rows = lambda a, *rest: a.reshape(BN, K, P, *rest)
    up_rows = lambda a, *rest: a.reshape(K, P, BN, *rest)
    down_gen = wdd.reshape(BN, K, n_chunk, ROWS, C).transpose(2, 1, 4, 3, 0)
    up_gen = wdu.reshape(K, P, n_chunk, ROWS, C).transpose(2, 0, 4, 3, 1)
    both = lambda a, b: np.stack([down_rows(a).transpose(2, 1, 0), up_rows(b).transpose(2, 0, 1)], axis=2)
    return {
        "x": x.reshape(TILES, P, D),
        "x_t": x.reshape(TILES, P, K, P).transpose(0, 3, 2, 1),
        "cond_t": cond.T,
        "norm_t": norm_w.T,
        "up_t": up_w.reshape(2 * FF, K, P).transpose(2, 1, 0),
        "down_t": down_w.reshape(D, FC, P).transpose(2, 1, 0),
        "gen_w": np.concatenate([down_gen, up_gen]).reshape(CHUNKS, P, ROWS * P),
        "base_w": both(wd, wu),
        "base_b": both(bdd, bdu),
        "down_bias": bd.reshape(BN, 1),
        "up_bias": bu.reshape(1, D),
    }


def kernel(x, cond_256, L0_cond_norm_w, L0_cond_up_w, L0_cond_down_w, L1_cond_Wd, L1_cond_bd, L1_cond_Wu,
           L1_cond_bu, L1_cond_Wdd, L1_cond_bdd, L1_cond_Wdu, L1_cond_bdu):
    import numpy as np
    import concourse.bacc as bacc
    from concourse.bass_utils import run_bass_kernel_spmd

    given = [np.asarray(a) for a in (x, cond_256, L0_cond_norm_w, L0_cond_up_w, L0_cond_down_w, L1_cond_Wd,
                                     L1_cond_bd, L1_cond_Wu, L1_cond_bu, L1_cond_Wdd, L1_cond_bdd, L1_cond_Wdu,
                                     L1_cond_bdu)]
    arrays = {name: np.ascontiguousarray(a) for name, a in layouts(np, *given).items()}
    nc = bacc.Bacc("TRN2", target_bir_lowering=False, num_devices=1)
    args = {name: nc.dram_tensor(f"in_{name}", a.shape, mybir.dt.from_np(a.dtype), kind="ExternalInput").ap()
            for name, a in arrays.items()}
    out = nc.dram_tensor("out", [TILES, P, D], F32, kind="ExternalOutput").ap()
    build(nc, **args, out=out)
    r = run_bass_kernel_spmd(nc, [{f"in_{name}": a for name, a in arrays.items()}], core_ids=[0])
    return r.results[0]["out"].reshape(BATCH, SEQ, D)
```

```python
from contextlib import ExitStack

import concourse.bass as bass
from concourse import mybir
from concourse.alu_op_type import AluOpType as ALU

ACT = mybir.ActivationFunctionType
AX = mybir.AxisListType
F32 = mybir.dt.float32
F32R = mybir.dt.float32r
BF16 = mybir.dt.bfloat16

P = 128
BATCH, SEQ, D, C = 64, 64, 256, 64
FF, BN = 1024, 128
TILES = BATCH * SEQ // P
K = D // P
PER = P // SEQ
FC = FF // P
HALF = FF // 2
ROWS = 4
CHUNKS = 2 * BN // ROWS
SLOTS = 4
MAKERS = CHUNKS // SLOTS
PAIRS = TILES // 2
UNITS = TILES // 2
UNIT_T, UNIT_B = 2, 2 * PER
SHIFT = 18
MAKE, PLAIN, MERGE = range(3)
ROUND = 12582912.0
QMAX = 127.0
DELTA = 0.1
WARM = 10
EPS = 1e-6
TINY = 1e-5
assert MAKERS % 2 == 0 and SHIFT == MAKERS + 2


def after(engine, semaphore, value):
    if not isinstance(value, int) or value > 0:
        engine.wait_ge(semaphore, value)


def build(nc, x, x_t, cond_t, norm_t, up_t, down_t, gen_w, base_w, base_b, down_bias, up_bias, out):
    scratch = nc.dram_tensor("layer1_weights", [BATCH, K, 2 * P, P], F32, kind="Internal").ap()

    with ExitStack() as ctx:
        def sb(name, shape, dt=F32):
            return ctx.enter_context(nc.sbuf_tensor(name, shape, dt))

        def sem(name):
            return ctx.enter_context(nc.semaphore(name))

        x_in = sb("x_in", [P, TILES, D])
        x1 = sb("x1", [P, 2, D])
        up_hi = sb("up_hi", [P, K, 2 * FF], F32R)
        up_lo = sb("up_lo", [P, K, 2 * FF], F32R)
        down_q = sb("down_q", [P, FC, D], BF16)
        norm_sb = sb("norm_sb", [C, D])
        scale_t = sb("scale_t", [P, K, BATCH])
        xt_in = sb("xt_in", [P, 2, K, P])
        h_all = sb("h_all", [P, K, P])
        h_hi = sb("h_hi", [P, 2, K, P], F32R)
        h_lo = sb("h_lo", [P, 2, K, P], F32R)
        gelu = sb("gelu", [P, 2, HALF])
        hid = sb("hid", [P, FF])
        quant = sb("quant", [P, FF], BF16)
        quant_t = sb("quant_t", [P, FC, P], BF16)
        square = sb("square", [P, D])
        meansq = sb("meansq", [P, 2])
        rms = sb("rms", [P, 2, 5])
        peak = sb("peak", [P, 2, 4])
        factor = sb("factor", [P, 2])
        numbers = sb("numbers", [P, 3])
        weight_sum = sb("weight_sum", [P, 4])
        ident_b = sb("ident_b", [P, P], BF16)
        ident = sb("ident", [P, P])
        ones = sb("ones", [P, P])
        cond2 = sb("cond2", [P, P])
        cond2_hi = sb("cond2_hi", [P, P], F32R)
        cond2_lo = sb("cond2_lo", [P, P], F32R)
        base = sb("base", [P, K, 2, P])
        base_raw = sb("base_raw", [P, 2, K, 2, P])
        down_relu = sb("down_relu", [P, UNIT_T * P])
        out_sb = sb("out_sb", [P, 2, K, UNIT_T * P])
        down_bias_sb = sb("down_bias_sb", [P, 1])
        up_bias_sb = sb("up_bias_sb", [P, K])

        with ExitStack() as start:
            up_raw = start.enter_context(nc.sbuf_tensor("up_raw", [P, K, 2 * FF], F32))
            down_raw = start.enter_context(nc.sbuf_tensor("down_raw", [P, FC, D], F32))
            down_size = start.enter_context(nc.sbuf_tensor("down_size", [P, FC, D], BF16))
        x1_t = sb("x1_t", [P, TILES, K, P])
        with ExitStack() as makers:
            chunk_in = makers.enter_context(nc.sbuf_tensor("chunk_in", [P, SLOTS, ROWS * P], F32))
            chunk_hi = makers.enter_context(nc.sbuf_tensor("chunk_hi", [P, SLOTS, ROWS * P], F32R))
            chunk_lo = makers.enter_context(nc.sbuf_tensor("chunk_lo", [P, SLOTS, ROWS * P], F32R))
            chunk_out = makers.enter_context(nc.sbuf_tensor("chunk_out", [P, SLOTS, ROWS * P], F32))
        delta_in = sb("delta_in", [P, 2, UNIT_B, K, 2, P])
        w1 = sb("w1", [P, 2, UNIT_B, K, 2, P])

        banks = [ctx.enter_context(nc.psum_tensor(f"bank{i}", [P, HALF], F32)) for i in range(4)]
        bank_t = ctx.enter_context(nc.psum_tensor("bank_t", [P, FC, P], BF16))
        bank_y = ctx.enter_context(nc.psum_tensor("bank_y", [P, HALF], F32))
        bank_g = [ctx.enter_context(nc.psum_tensor(f"bank_g{i}", [P, HALF], F32)) for i in range(2)]
        gate_ps, val_ps = [banks[0], banks[2]], [banks[1], banks[3]]
        y_ps = bank_y[:, 0:D]
        x1_t_ps = bank_y[:, D:2 * D]
        down_ps = bank_g[0][:, 0:UNIT_T * P]
        up_ps = bank_g[1][:].rearrange("p (k c) -> p k c", k=K)

        cond_in, norm_in, down_in = sem("cond_in"), sem("norm_in"), sem("down_in")
        up_in = [sem(f"up_in{n}") for n in range(4)]
        small_in = sem("small_in")
        x_here = [sem(f"x_here{p}") for p in range(2)]
        xt_here = [sem(f"xt_here{p}") for p in range(2)]
        cleared, identity_made, ones_made = sem("cleared"), sem("identity_made"), sem("ones_made")
        identf_made, numbers_made = sem("identf_made"), sem("numbers_made")
        scale_ready, scale_made = sem("scale_ready"), sem("scale_made")
        cond_hi_made, cond_split = sem("cond_hi_made"), sem("cond_split")
        up_hi_made, up_lo_made = sem("up_hi_made"), sem("up_lo_made")
        weights_summed, weights_total = sem("weights_summed"), sem("weights_total")
        weight_steps, down_q_made = sem("weight_steps"), sem("down_q_made")
        table_loaded = sem("table_loaded")
        base_steps = sem("base_steps")
        chunk_here = [sem(f"chunk_here{s}") for s in range(SLOTS)]
        chunk_stored = [sem(f"chunk_stored{s}") for s in range(SLOTS)]
        chunk_hi_made = sem("chunk_hi_made")
        chunk_split = [sem(f"chunk_split{s}") for s in range(SLOTS)]
        chunk_made, chunk_copied = sem("chunk_made"), sem("chunk_copied")
        h_scaled, h_hi_made, h_split = sem("h_scaled"), sem("h_hi_made"), sem("h_split")
        gate_ready, val_ready = sem("gate_ready"), sem("val_ready")
        squared, rms_steps = sem("squared"), sem("rms_steps")
        gelu_done, hid_made, peak_steps = sem("gelu_done"), sem("hid_made"), sem("peak_steps")
        hid_rounded, quant_made = sem("hid_rounded"), sem("quant_made")
        quant_turned, quant_copied = sem("quant_turned"), sem("quant_copied")
        y_ready, factor_made, x1_made = sem("y_ready"), sem("factor_made"), sem("x1_made")
        delta_here = [[sem(f"delta_here{p}{j}") for j in range(UNIT_T)] for p in range(2)]
        w1_made, x1_turned, x1_copied = sem("w1_made"), sem("x1_turned"), sem("x1_copied")
        down_ready, relu_done = sem("down_ready"), sem("relu_done")
        up_ready, out_made = sem("up_ready"), sem("out_made")
        out_stored = [sem(f"out_stored{p}") for p in range(2)]

        RMS_STEPS, PEAK_STEPS = 7, 4
        PIECES = [(FF + 0, FF + HALF), (0, HALF), (FF + HALF, 2 * FF), (HALF, FF)]
        block = ctx.enter_context(nc.Block())

        def pair_of_tiles(step, pair, kind):
            for p in range(2):
                step(pair * 2 + p, pair, p, kind)

        def walk0(engine, step, between=None):
            pair_of_tiles(step, 0, MAKE)
            with engine.Fori(1, MAKERS // 2 - 1) as pair:
                pair_of_tiles(step, pair, MAKE)
            pair_of_tiles(step, MAKERS // 2 - 1, MAKE)
            if between:
                between()
            pair_of_tiles(step, MAKERS // 2, PLAIN)
            pair_of_tiles(step, SHIFT // 2, MERGE)
            with engine.Fori(SHIFT // 2 + 1, PAIRS - 1) as pair:
                pair_of_tiles(step, pair, MERGE)
            pair_of_tiles(step, PAIRS - 1, MERGE)

        def is_tile(t, *which):
            return isinstance(t, int) and t in which

        def splits(t, kind):
            return kind == MAKE and not is_tile(t, MAKERS - 1)

        def tile_of(tensor, t):
            return tensor[:, bass.ds(t, 1)].rearrange("p t d -> p (t d)")

        @block.sync
        def _(sp):
            def load_chunk(t, c):
                sp.dma_start(chunk_in[:, c, :], gen_w[t * SLOTS + c]).then_inc(chunk_here[c], 16)

            def reload_chunk(t, c):
                sp.wait_ge(chunk_split[c], t)
                load_chunk(t, c)

            def store_chunk(t, c):
                q = t * SLOTS + c
                sp.wait_ge(chunk_copied, q + 1)
                target = scratch[:, :, bass.ds(q * ROWS, ROWS), :].rearrange("b k r c -> k b (r c)")
                sp.dma_start(target, chunk_out[:, c, :]).then_inc(chunk_stored[c], 16)

            def load_x_t(t, p):
                after(sp, h_split, t - 1)
                sp.dma_start(xt_in[:, p], x_t[t]).then_inc(xt_here[p], 16)

            def load_x(t, p):
                after(sp, squared, t - 1)
                sp.dma_start(tile_of(x_in, t), x[t]).then_inc(x_here[p], 16)

            def load_up(n):
                a, b = PIECES[n]
                sp.dma_start(up_raw[:, :, a:b], up_t[:, :, a:b]).then_inc(up_in[n], 16)

            def load_delta(u, q):
                after(sp, w1_made, (u - 1) * UNIT_T)
                for j in range(UNIT_T):
                    sp.dma_start(delta_in[:, q, j * PER:(j + 1) * PER].rearrange("p b k m c -> p (b k m) c"),
                                 scratch[bass.ds(u * UNIT_B + j * PER, PER)]
                                 .rearrange("b k (m r) c -> r (b k m) c", m=2)).then_inc(delta_here[q][j], 16)

            def store_out(u, q):
                sp.wait_ge(out_made, (u + 1) * UNIT_T * K)
                sp.dma_start(out[u], out_sb[:, q].rearrange("p k c -> p (k c)")).then_inc(out_stored[q], 16)

            load_up(0)
            load_chunk(0, 0)
            sp.wait_ge(cleared, 1)
            for k in range(K):
                sp.dma_start(cond2[k * C:(k + 1) * C, k * BATCH:(k + 1) * BATCH], cond_t).then_inc(cond_in, 16)
            sp.dma_start(norm_sb[:], norm_t).then_inc(norm_in, 16)
            load_x_t(0, 0)
            load_up(1)
            load_x(0, 0)
            load_chunk(0, 1)
            load_up(2)
            load_chunk(0, 2)
            load_up(3)
            load_chunk(0, 3)
            load_x_t(1, 1)
            load_x(1, 1)
            sp.dma_start(down_raw[:], down_t).then_inc(down_in, 16)
            for c in range(SLOTS):
                reload_chunk(1, c)

            def step(t, pair, p, kind):
                if not is_tile(t, TILES - 2, TILES - 1):
                    load_x_t(t + 2, p)
                    load_x(t + 2, p)
                if is_tile(t, 0):
                    for c in range(SLOTS):
                        store_chunk(0, c)
                    for c in range(SLOTS):
                        reload_chunk(2, c)
                elif kind == MAKE:
                    for c in range(SLOTS):
                        store_chunk(t, c)
                        if splits(t, kind) and not is_tile(t, MAKERS - 2):
                            reload_chunk(t + 2, c)
                if is_tile(t, MAKERS - 2):
                    for target, source in ((base_raw[:, 0], base_w), (base_raw[:, 1], base_b),
                                           (down_bias_sb[:], down_bias), (up_bias_sb[:], up_bias)):
                        sp.dma_start(target, source).then_inc(small_in, 16)
                if is_tile(t, MAKERS):
                    load_delta(0, 0)
                    load_delta(1, 1)
                elif kind != MAKE and not is_tile(t, TILES - 1):
                    load_delta(t - SHIFT + 3, 1 - p)
                if kind == MERGE:
                    store_out(t - SHIFT, p)

            def all_chunks_stored():
                for c in range(SLOTS):
                    sp.wait_ge(chunk_stored[c], 16 * MAKERS)

            walk0(sp, step, all_chunks_stored)
            store_out(UNITS - 2, 0)
            for j in range(UNIT_T):
                sp.wait_ge(out_made, (TILES - UNIT_T + j + 1) * K)
                cols = slice(j * P, (j + 1) * P)
                sp.dma_start(out[UNITS - 1].rearrange("p (k c) -> p k c", k=K)[:, :, cols], out_sb[:, 1, :, cols]
                             ).then_inc(out_stored[1], 16)
            sp.wait_ge(out_stored[0], 16 * UNITS // 2)
            sp.wait_ge(out_stored[1], 16 * (UNITS // 2 + 1))

        @block.gpsimd
        def _(pool):
            pool.memset(cond2[:], 0.0).then_inc(cleared, 1)
            pool.memset(ident[:], 0.0).then_inc(cleared, 1)
            minus_half, eps, one_half = (numbers[:, n:n + 1] for n in range(3))
            for place, value in ((minus_half, -0.5), (eps, EPS), (one_half, 1.5)):
                pool.memset(place, value).then_inc(numbers_made, 1)
            pool.memset(ones[:], 1.0).then_inc(ones_made, 1)
            pool.wait_ge(cleared, 2)
            pool.affine_select(out=ident[:], in_=ident[:], compare_op=ALU.not_equal, fill=1.0, base=0,
                               pattern=[[-1, P]], channel_multiplier=1).then_inc(identf_made, 1)
            pool.wait_ge(identf_made, 1)
            pool.tensor_copy(ident_b[:], ident[:]).then_inc(identity_made, 1)
            pool.wait_ge(numbers_made, 3)

            def root(t, p):
                v, guess, sq, fix, r = (rms[:, p, n:n + 1] for n in range(5))
                done = t * RMS_STEPS
                pool.wait_ge(squared, t + 1)
                after(pool, peak_steps, (t - 1) * PEAK_STEPS)
                for n, (result, one, other, op) in enumerate((
                        (v, meansq[:, p:p + 1], eps, ALU.add), (guess, v, minus_half, ALU.pow),
                        (sq, guess, guess, ALU.mult), (sq, sq, v, ALU.mult), (fix, sq, minus_half, ALU.mult),
                        (fix, fix, one_half, ALU.add), (r, guess, fix, ALU.mult))):
                    if n:
                        pool.wait_ge(rms_steps, done + n)
                    pool.tensor_tensor(result, one, other, op).then_inc(rms_steps, 1)

            def split_chunk(t, c):
                pool.wait_ge(chunk_hi_made, t * SLOTS + c + 1)
                pool.tensor_tensor(chunk_lo[:, c, :], chunk_in[:, c, :], chunk_hi[:, c, :].bitcast(F32),
                                   ALU.subtract).then_inc(chunk_split[c], 1)

            def share():
                pool.wait_ge(small_in, 64)
                pool.tensor_scalar(base[:], base_raw[:, 1], DELTA, None, ALU.mult).then_inc(base_steps, 1)
                pool.wait_ge(base_steps, 1)
                pool.tensor_tensor(base[:], base[:], base_raw[:, 0], ALU.add).then_inc(base_steps, 1)

            def make_w1(u, q, eights):
                after(pool, up_ready, (u - 1) * UNIT_T)
                shared = base[:].rearrange("p k m c -> p (k m c)").unsqueeze(1).to_broadcast([P, PER, K * 2 * P])
                for j in range(UNIT_T):
                    pool.wait_ge(delta_here[q][j], (eights + 1) * 16)
                    of_tile = slice(j * PER, (j + 1) * PER)
                    pool.tensor_tensor(w1[:, q, of_tile].rearrange("p b k m c -> p b (k m c)"),
                                       delta_in[:, q, of_tile].rearrange("p b k m c -> p b (k m c)"), shared,
                                       ALU.add).then_inc(w1_made, 1)

            def step(t, pair, p, kind):
                if splits(t, kind) and not is_tile(t, 0):
                    split_chunk(t + 1, 1)
                if is_tile(t, MAKERS):
                    share()
                    pool.wait_ge(base_steps, 2)
                if kind != MAKE and not is_tile(t, MAKERS):
                    make_w1(t - SHIFT + 1, 1 - p, pair - SHIFT // 2 + p)
                if not is_tile(t, TILES - 1):
                    root(t + 1, 1 - p)
                if is_tile(t, 0):
                    for c in range(SLOTS):
                        split_chunk(t + 1, c)
                elif splits(t, kind):
                    split_chunk(t + 1, 3)

            split_chunk(0, 0)
            split_chunk(0, 1)
            root(0, 0)
            split_chunk(0, 3)
            walk0(pool, step)
            make_w1(UNITS - 1, 1, UNITS // 2 - 1)

        @block.scalar
        def _(act):
            def high_chunk(t, c):
                q = t * SLOTS + c
                act.wait_ge(chunk_here[c], (t + 1) * 16)
                after(act, chunk_made, q - SLOTS + 1)
                act.copy(chunk_hi[:, c, :], chunk_in[:, c, :]).then_inc(chunk_hi_made, 1)

            def copy_chunk(t, c):
                act.wait_ge(chunk_made, t * SLOTS + c + 1)
                after(act, chunk_stored[c], t * 16)
                act.copy(chunk_out[:, c, :], bank_g[c % 2][:]).then_inc(chunk_copied, 1)

            def mean_squares(t, pair, p):
                act.wait_ge(x_here[p], (pair + 1) * 16)
                after(act, rms_steps, (t - 2) * RMS_STEPS + 1)
                after(act, squared, t)
                act.activation(square[:], tile_of(x_in, t), ACT.Square, scale=D ** -0.5,
                               accum_out=meansq[:, p:p + 1]).then_inc(squared, 1)

            def copy_quant(t):
                act.wait_ge(quant_turned, t + 1)
                after(act, y_ready, t)
                for n in range(2):
                    blocks = slice(n * FC // 2, (n + 1) * FC // 2)
                    act.copy(quant_t[:, blocks, :], bank_t[:, blocks, :]).then_inc(quant_copied, 1)

            def copy_x1(t):
                act.wait_ge(x1_turned, t + 1)
                act.copy(x1_t[:, bass.ds(t, 1)].rearrange("p t k c -> p (t k c)"), x1_t_ps).then_inc(x1_copied, 1)

            def high_up(n):
                a, b = PIECES[n]
                act.wait_ge(up_in[n], 16)
                for k in range(K):
                    act.copy(up_hi[:, k, a:b], up_raw[:, k, a:b]).then_inc(up_hi_made, 1)

            def relu(u, tiles=range(UNIT_T)):
                act.wait_ge(down_ready, u * UNIT_T + tiles[-1] + 1)
                after(act, up_ready, u * UNIT_T)
                cols = slice(tiles[0] * P, (tiles[-1] + 1) * P)
                act.activation(down_relu[:, cols], down_ps[:, cols], ACT.Relu, bias=down_bias_sb[:]
                               ).then_inc(relu_done, len(tiles))

            def first_tile():
                act.wait_ge(numbers_made, 1)
                act.activation(square[:, 0:1], numbers[:, 0:1], ACT.Gelu).then_inc(table_loaded, 1)
                high_up(0)
                high_chunk(0, 0)
                act.wait_ge(cond_in, 32)
                act.activation(cond2_hi[:], cond2[:], ACT.Copy, scale=DELTA).then_inc(cond_hi_made, 1)
                high_up(1)
                high_chunk(0, 1)
                act.wait_ge(table_loaded, 1)
                mean_squares(0, 0, 0)
                copy_chunk(0, 0)
                high_up(2)
                high_chunk(0, 2)
                high_up(3)
                high_chunk(0, 3)
                gelu_half(0, 0, 0)
                copy_chunk(0, 1)
                mean_squares(1, 0, 1)
                gelu_half(0, 0, 1)
                copy_chunk(0, 2)
                act.wait_ge(down_in, 16)
                act.activation(down_size[:], down_raw[:], ACT.Abs, accum_out=weight_sum[:, 0:1]
                               ).then_inc(weights_summed, 1)
                high_chunk(1, 0)
                high_chunk(1, 1)

            def gelu_half(t, p, half):
                act.wait_ge(gate_ready, t * 2 + half + 1)
                if half == 0:
                    act.wait_ge(rms_steps, (t + 1) * RMS_STEPS)
                after(act, hid_made, t * 2 + half - 1)
                act.activation(gelu[:, half, :], gate_ps[half][:], ACT.Gelu, scale=rms[:, p, 4:5]
                               ).then_inc(gelu_done, 1)

            def copy_and_high(t, kind, slots):
                for c in slots:
                    copy_chunk(t, c)
                if splits(t, kind):
                    for c in slots:
                        high_chunk(t + 1, c)

            def step(t, pair, p, kind):
                if is_tile(t, 0):
                    first_tile()
                    return
                if is_tile(t, SHIFT):
                    act.wait_ge(small_in, 64)
                gelu_half(t, p, 0)
                if is_tile(t, 1):
                    copy_chunk(0, 3)
                    high_chunk(1, 2)
                    high_chunk(1, 3)
                elif kind == MAKE:
                    copy_and_high(t, kind, range(SLOTS // 2))
                if kind == MERGE:
                    relu(t - SHIFT)
                gelu_half(t, p, 1)
                if kind == PLAIN:
                    copy_x1(t - 2)
                    copy_quant(t - 1)
                if not is_tile(t, TILES - 1):
                    mean_squares(t + 1, pair + p, 1 - p)
                if is_tile(t, 1):
                    copy_chunk(1, 0)
                    copy_chunk(1, 1)
                    copy_quant(0)
                    high_chunk(2, 0)
                    high_chunk(2, 1)
                elif kind != PLAIN:
                    copy_x1(t - 2)
                    copy_quant(t - 1)
                if kind == MAKE:
                    copy_and_high(t, kind, range(SLOTS // 2, SLOTS))

            walk0(act, step)
            relu(UNITS - 2)
            copy_quant(TILES - 1)
            copy_x1(TILES - 2)
            relu(UNITS - 1, range(0, 1))
            copy_x1(TILES - 1)
            relu(UNITS - 1, range(1, 2))

        @block.vector
        def _(dve):
            def split(t, pair, p):
                dve.wait_ge(xt_here[p], (pair + 1) * 16)
                after(dve, h_split, t)
                dve.tensor_tensor(h_all[:].rearrange("p k (b l) -> p k b l", b=PER),
                                  xt_in[:, p].rearrange("p k (b l) -> p k b l", b=PER),
                                  scale_t[:, :, bass.ds(t * PER, PER)].unsqueeze(3).to_broadcast([P, K, PER, SEQ]),
                                  ALU.mult).then_inc(h_scaled, 1)
                dve.wait_ge(h_scaled, t + 1)
                after(dve, val_ready, 2 * (t - 1))
                dve.tensor_copy(h_hi[:, p], h_all[:]).then_inc(h_hi_made, 1)
                dve.wait_ge(h_hi_made, t + 1)
                dve.tensor_tensor(h_lo[:, p], h_all[:], h_hi[:, p].bitcast(F32), ALU.subtract).then_inc(h_split, 1)

            def split_chunk(t, c):
                dve.wait_ge(chunk_hi_made, t * SLOTS + c + 1)
                dve.tensor_tensor(chunk_lo[:, c, :], chunk_in[:, c, :], chunk_hi[:, c, :].bitcast(F32),
                                  ALU.subtract).then_inc(chunk_split[c], 1)

            def split_up(n):
                a, b = PIECES[n]
                for k in range(K):
                    dve.wait_ge(up_hi_made, n * K + k + 1)
                    dve.tensor_tensor(up_lo[:, k, a:b], up_raw[:, k, a:b], up_hi[:, k, a:b].bitcast(F32),
                                      ALU.subtract).then_inc(up_lo_made, 1)

            def gate(t, half):
                dve.wait_ge(gelu_done, t * 2 + half + 1)
                dve.wait_ge(val_ready, t * 2 + half + 1)
                after(dve, quant_made, t)
                dve.tensor_tensor(hid[:, half * HALF:(half + 1) * HALF], gelu[:, half, :], val_ps[half][:],
                                  ALU.mult).then_inc(hid_made, 1)

            def find_peak(t, p):
                dve.wait_ge(hid_made, t * 2 + 2)
                dve.tensor_reduce(peak[:, p, 0:1], hid[:], AX.X, ALU.max, apply_absolute_value=True
                                  ).then_inc(peak_steps, 1)

            def quantise(t, p):
                top, clipped, inverse, scale = (peak[:, p, n:n + 1] for n in range(4))
                r, done = rms[:, p, 4:5], t * PEAK_STEPS
                dve.wait_ge(rms_steps, (t + 1) * RMS_STEPS)
                dve.wait_ge(peak_steps, done + 1)
                dve.tensor_scalar(clipped, top, r, TINY, ALU.mult, ALU.max).then_inc(peak_steps, 1)
                dve.wait_ge(peak_steps, done + 2)
                dve.reciprocal(inverse, clipped).then_inc(peak_steps, 1)
                dve.wait_ge(peak_steps, done + 3)
                dve.tensor_scalar(scale, inverse, r, QMAX, ALU.mult, ALU.mult).then_inc(peak_steps, 1)
                dve.wait_ge(peak_steps, done + 4)
                dve.tensor_scalar(hid[:], hid[:], scale, ROUND, ALU.mult, ALU.add).then_inc(hid_rounded, 1)
                dve.wait_ge(hid_rounded, t + 1)
                after(dve, quant_turned, t)
                dve.tensor_scalar(quant[:], hid[:], ROUND, QMAX, ALU.subtract, ALU.min).then_inc(quant_made, 1)

            def worth(t, p):
                dve.wait_ge(peak_steps, t * PEAK_STEPS + 2)
                dve.tensor_scalar(factor[:, p:p + 1], peak[:, p, 1:2], weight_sum[:, 2:3], 1.0 / QMAX,
                                  ALU.mult, ALU.mult).then_inc(factor_made, 1)

            def residual(t, p):
                dve.wait_ge(factor_made, t + 1)
                dve.wait_ge(y_ready, t + 1)
                dve.scalar_tensor_tensor(out=x1[:, p, :], in0=y_ps, scalar=factor[:, p:p + 1], in1=tile_of(x_in, t),
                                         op0=ALU.mult, op1=ALU.add).then_inc(x1_made, 1)

            def finish(u, q, eights, tiles=range(UNIT_T)):
                dve.wait_ge(up_ready, u * UNIT_T + tiles[-1] + 1)
                after(dve, out_stored[q], eights * 16)
                n, cols = len(tiles), slice(tiles[0] * P, (tiles[-1] + 1) * P)
                for k in range(K):
                    dve.scalar_tensor_tensor(
                        out=out_sb[:, q, k, cols].rearrange("p (j c) -> p j c", j=n),
                        in0=up_ps[:, k, cols].rearrange("p (j c) -> p j c", j=n), scalar=up_bias_sb[:, k:k + 1],
                        in1=x1_t[:, bass.ds(u * UNIT_T + tiles[0], n), k, :], op0=ALU.add, op1=ALU.add
                    ).then_inc(out_made, n)

            def weight_scale():
                dve.wait_ge(weights_total, 1)
                dve.tensor_scalar(weight_sum[:, 2:3], bank_y[:, 0:1], 1.0 / (D * FF), TINY, ALU.mult, ALU.max
                                  ).then_inc(weight_steps, 1)
                dve.wait_ge(weight_steps, 1)
                dve.reciprocal(weight_sum[:, 3:4], weight_sum[:, 2:3]).then_inc(weight_steps, 1)

            def round_weights():
                w = down_raw[:].rearrange("p c d -> p (c d)")
                dve.wait_ge(weight_steps, 2)
                dve.tensor_scalar(w, w, weight_sum[:, 3:4], ROUND, ALU.mult, ALU.add).then_inc(weight_steps, 1)

            def quantise_weights():
                w, w_q = (tensor[:].rearrange("p c d -> p (c d)") for tensor in (down_raw, down_q))
                dve.wait_ge(weight_steps, 3)
                dve.tensor_scalar(w_q, w, ROUND, 1.0, ALU.subtract, ALU.min).then_inc(weight_steps, 1)
                dve.wait_ge(weight_steps, 4)
                dve.tensor_scalar(w_q, w_q, -1.0, None, ALU.max).then_inc(down_q_made, 1)

            def first_tile():
                split_up(0)
                dve.wait_ge(cond_hi_made, 1)
                dve.scalar_tensor_tensor(out=cond2_lo[:], in0=cond2[:], scalar=DELTA, in1=cond2_hi[:].bitcast(F32),
                                         op0=ALU.mult, op1=ALU.subtract).then_inc(cond_split, 1)
                dve.wait_ge(scale_ready, 1)
                dve.tensor_scalar(scale_t[:].rearrange("p k b -> p (k b)"), bank_y[:, 0:K * BATCH], 1.0, None,
                                  ALU.add).then_inc(scale_made, 1)
                dve.wait_ge(scale_made, 1)
                split(0, 0, 0)
                split_up(1)
                split_up(2)
                split_chunk(0, 2)
                split_up(3)
                split(1, 0, 1)
                gate(0, 0)
                gate(0, 1)
                find_peak(0, 0)
                quantise(0, 0)
                weight_scale()
                worth(0, 0)

            def step(t, pair, p, kind):
                if is_tile(t, 0):
                    first_tile()
                    return
                if is_tile(t, 1):
                    round_weights()
                    quantise_weights()
                gate(t, 0)
                if not is_tile(t, TILES - 1):
                    split(t + 1, pair + p, 1 - p)
                gate(t, 1)
                if splits(t, kind):
                    split_chunk(t + 1, 0)
                find_peak(t, p)
                quantise(t, p)
                worth(t, p)
                residual(t - 1, 1 - p)
                if splits(t, kind):
                    split_chunk(t + 1, 2)
                if is_tile(t, SHIFT):
                    dve.wait_ge(small_in, 64)
                if kind == MERGE:
                    finish(t - SHIFT, p, pair - SHIFT // 2)

            walk0(dve, step)
            finish(UNITS - 2, 0, UNITS // 2 - 1)
            residual(TILES - 1, 1)
            for j in range(UNIT_T):
                finish(UNITS - 1, 1, UNITS // 2 - 1, range(j, j + 1))

        @block.tensor
        def _(pe):
            def make_chunk(t, c):
                pe.wait_ge(chunk_split[c], t + 1)
                after(pe, chunk_copied, t * SLOTS + c - 1)
                product = bank_g[c % 2][:]
                pe.matmul(product, cond2_lo[:], chunk_hi[:, c, :], start=True, stop=False)
                pe.matmul(product, cond2_hi[:], chunk_lo[:, c, :], start=False, stop=False)
                pe.matmul(product, cond2_hi[:], chunk_hi[:, c, :], start=False, stop=True).then_inc(chunk_made, 1)

            def up_product(t, p, half, n):
                bank, first_col, ready, used = ((gate_ps[half], FF + half * HALF, gate_ready, gelu_done),
                                                (val_ps[half], half * HALF, val_ready, hid_made))[n]
                pe.wait_ge(h_split, t + 1)
                after(pe, used, t * 2 + half - 1)
                cols = slice(first_col, first_col + HALF)
                for k in range(K):
                    if is_tile(t, 0):
                        pe.wait_ge(up_lo_made, (2 * half + n) * K + k + 1)
                    hi, lo = h_hi[:, p, k, :], h_lo[:, p, k, :]
                    pe.matmul(bank[:], lo, up_hi[:, k, cols], start=(k == 0), stop=False)
                    pe.matmul(bank[:], hi, up_lo[:, k, cols], start=False, stop=False)
                    last = pe.matmul(bank[:], hi, up_hi[:, k, cols], start=False, stop=(k == K - 1))
                last.then_inc(ready, 1)

            def turn_quant(t):
                pe.wait_ge(quant_made, t + 1)
                after(pe, quant_copied, t * 2)
                for c in range(FC):
                    last = pe.transpose(bank_t[:, c, :], quant[:, c * P:(c + 1) * P], ident_b[:])
                last.then_inc(quant_turned, 1)

            def down_project(t):
                after(pe, x1_made, t)
                after(pe, x1_copied, t)
                for c in range(FC):
                    if c % (FC // 2) == 0:
                        pe.wait_ge(quant_copied, t * 2 + 1 + c // (FC // 2))
                    last = pe.matmul(y_ps, quant_t[:, c, :], down_q[:, c, :], start=(c == 0), stop=(c == FC - 1))
                last.then_inc(y_ready, 1)

            def turn_x1(t, p):
                pe.wait_ge(x1_made, t + 1)
                for k in range(K):
                    last = pe.transpose(x1_t_ps[:, k * P:(k + 1) * P], x1[:, p, k * P:(k + 1) * P], ident[:])
                last.then_inc(x1_turned, 1)

            def down_unit(u, q, tiles=range(UNIT_T)):
                after(pe, relu_done, u * UNIT_T + tiles[0])
                for j in tiles:
                    pe.wait_ge(w1_made, u * UNIT_T + j + 1)
                    pe.wait_ge(x1_copied, u * UNIT_T + j + 1)
                    for b in range(PER):
                        s = j * PER + b
                        for k in range(K):
                            tokens = x1_t[:, bass.ds(u * UNIT_T + j, 1), k, b * SEQ:(b + 1) * SEQ]
                            last = pe.matmul(down_ps[:, s * SEQ:(s + 1) * SEQ], w1[:, q, s, k, 0, :],
                                             tokens.rearrange("p t c -> p (t c)"), start=(k == 0), stop=(k == K - 1))
                last.then_inc(down_ready, len(tiles))

            def up_unit(u, q, tiles=range(UNIT_T)):
                pe.wait_ge(relu_done, u * UNIT_T + tiles[-1] + 1)
                after(pe, out_made, (u * UNIT_T + tiles[0]) * K)
                for s in range(tiles[0] * PER, (tiles[-1] + 1) * PER):
                    of_sequence = slice(s * SEQ, (s + 1) * SEQ)
                    for k in range(K):
                        last = pe.matmul(up_ps[:, k, of_sequence], w1[:, q, s, k, 1, :], down_relu[:, of_sequence],
                                         start=True, stop=True)
                last.then_inc(up_ready, len(tiles))

            def keep_warm(n):
                for _ in range(n):
                    pe.matmul(banks[3][:, 0:P], ones[:], ones[:], start=True, stop=True)

            def first_tile():
                pe.wait_ge(ones_made, 1)
                keep_warm(WARM)
                pe.wait_ge(cond_in, 32)
                pe.wait_ge(norm_in, 16)
                for k in range(K):
                    last = pe.matmul(bank_y[:, k * BATCH:(k + 1) * BATCH], norm_sb[:, k * P:(k + 1) * P],
                                     cond2[0:C, 0:BATCH], start=True, stop=True)
                last.then_inc(scale_ready, 1)
                pe.wait_ge(cond_split, 1)
                make_chunk(0, 0)
                up_product(0, 0, 0, 0)
                up_product(0, 0, 0, 1)
                make_chunk(0, 1)
                up_product(0, 0, 1, 0)
                make_chunk(0, 2)
                up_product(0, 0, 1, 1)
                make_chunk(0, 3)

            def total_weights():
                pe.wait_ge(weights_summed, 1)
                pe.wait_ge(scale_made, 1)
                pe.matmul(bank_y[:, 0:1], ones[:], weight_sum[:, 0:1], start=True, stop=True
                          ).then_inc(weights_total, 1)

            def step(t, pair, p, kind):
                if is_tile(t, 0):
                    first_tile()
                    return
                up_product(t, p, 0, 0)
                up_product(t, p, 0, 1)
                if kind == MAKE and not is_tile(t, 1):
                    make_chunk(t, 0)
                    make_chunk(t, 1)
                if kind == MERGE:
                    down_unit(t - SHIFT, p)
                up_product(t, p, 1, 0)
                if is_tile(t, 1):
                    total_weights()
                    pe.wait_ge(identity_made, 1)
                if kind == PLAIN:
                    turn_x1(t - 2, p)
                    turn_quant(t - 1)
                up_product(t, p, 1, 1)
                if is_tile(t, 1):
                    make_chunk(t, 0)
                    make_chunk(t, 1)
                elif kind != PLAIN:
                    turn_x1(t - 2, p)
                if kind != PLAIN:
                    turn_quant(t - 1)
                if kind == MAKE:
                    make_chunk(t, 2)
                    make_chunk(t, 3)
                if kind == MERGE:
                    up_unit(t - SHIFT, p)
                if is_tile(t, 1):
                    pe.wait_ge(down_q_made, 1)
                down_project(t - 1)

            walk0(pe, step)
            down_unit(UNITS - 2, 0)
            turn_quant(TILES - 1)
            turn_x1(TILES - 2, 0)
            up_unit(UNITS - 2, 0)
            down_project(TILES - 1)
            down_unit(UNITS - 1, 1, range(0, 1))
            turn_x1(TILES - 1, 1)
            up_unit(UNITS - 1, 1, range(0, 1))
            down_unit(UNITS - 1, 1, range(1, 2))
            up_unit(UNITS - 1, 1, range(1, 2))


def layouts(np, x, cond, norm_w, up_w, down_w, wd, bd, wu, bu, wdd, bdd, wdu, bdu):
    n_chunk = CHUNKS // 2
    down_rows = lambda a, *rest: a.reshape(BN, K, P, *rest)
    up_rows = lambda a, *rest: a.reshape(K, P, BN, *rest)
    down_gen = wdd.reshape(BN, K, n_chunk, ROWS, C).transpose(2, 1, 4, 3, 0)
    up_gen = wdu.reshape(K, P, n_chunk, ROWS, C).transpose(2, 0, 4, 3, 1)
    both = lambda a, b: np.stack([down_rows(a).transpose(2, 1, 0), up_rows(b).transpose(2, 0, 1)], axis=2)
    return {
        "x": x.reshape(TILES, P, D),
        "x_t": x.reshape(TILES, P, K, P).transpose(0, 3, 2, 1),
        "cond_t": cond.T,
        "norm_t": norm_w.T,
        "up_t": up_w.reshape(2 * FF, K, P).transpose(2, 1, 0),
        "down_t": down_w.reshape(D, FC, P).transpose(2, 1, 0),
        "gen_w": np.concatenate([down_gen, up_gen]).reshape(CHUNKS, P, ROWS * P),
        "base_w": both(wd, wu),
        "base_b": both(bdd, bdu),
        "down_bias": bd.reshape(BN, 1),
        "up_bias": bu.reshape(K, P).T,
    }


def kernel(x, cond_256, L0_cond_norm_w, L0_cond_up_w, L0_cond_down_w, L1_cond_Wd, L1_cond_bd, L1_cond_Wu,
           L1_cond_bu, L1_cond_Wdd, L1_cond_bdd, L1_cond_Wdu, L1_cond_bdu):
    import numpy as np
    import concourse.bacc as bacc
    from concourse.bass_utils import run_bass_kernel_spmd

    given = [np.asarray(a) for a in (x, cond_256, L0_cond_norm_w, L0_cond_up_w, L0_cond_down_w, L1_cond_Wd,
                                     L1_cond_bd, L1_cond_Wu, L1_cond_bu, L1_cond_Wdd, L1_cond_bdd, L1_cond_Wdu,
                                     L1_cond_bdu)]
    arrays = {name: np.ascontiguousarray(a) for name, a in layouts(np, *given).items()}
    nc = bacc.Bacc("TRN2", target_bir_lowering=False, num_devices=1)
    args = {name: nc.dram_tensor(f"in_{name}", a.shape, mybir.dt.from_np(a.dtype), kind="ExternalInput").ap()
            for name, a in arrays.items()}
    out = nc.dram_tensor("out", [UNITS, P, K * UNIT_T * P], F32, kind="ExternalOutput").ap()
    build(nc, **args, out=out)
    r = run_bass_kernel_spmd(nc, [{f"in_{name}": a for name, a in arrays.items()}], core_ids=[0])
    return r.results[0]["out"].reshape(UNITS, P, K, UNIT_T * P).transpose(0, 3, 2, 1).reshape(BATCH, SEQ, D)
```
